# Optimizing a Trainium2 kernel written in Bass

```python
import numpy as np
import jax
import jax.numpy as jnp

def _softmax(x, axis=-1):
    return jax.nn.softmax(x, axis=axis)

def _gelu(x):
    return jax.nn.gelu(x, approximate=True)

def _silu(x):
    return jax.nn.silu(x)

def _sigmoid(x):
    return jax.nn.sigmoid(x)

def _layernorm(x, axis=-1, eps=1e-05):
    m = jnp.mean(x, axis=axis, keepdims=True)
    v = jnp.var(x, axis=axis, keepdims=True)
    return (x - m) / jnp.sqrt(v + eps)

def _scatter_add(tgt, idx, src, axis=0):
    return tgt.at[idx].add(src)

def _segment_sum(src, seg, n):
    return jax.ops.segment_sum(src, seg, n)
kernel_name = 'mk_macaron_d1_jaxref_r8_b61415'

def setup_inputs(seed: int=0):
    np.random.seed(seed)
    _w = jnp.asarray

    def _L0_attn_setup():
        import jax, jax.numpy as jnp
        import numpy as np
        NUM_HEADS = 16
        HEAD_DIM = 64
        NEG_INF = -1000000000.0

        def rotary_embedding(x, seq_len, head_dim):
            positions = jnp.arange(seq_len)
            dim_pairs = jnp.arange(0, head_dim, 2)
            freqs = 1.0 / 10000.0 ** (dim_pairs / head_dim)
            angles = positions[:, None] * freqs[None, :]
            cos = jnp.cos(angles)[:, None, :]
            sin = jnp.sin(angles)[:, None, :]
            x1 = x[..., ::2]
            x2 = x[..., 1::2]
            out1 = x1 * cos - x2 * sin
            out2 = x1 * sin + x2 * cos
            return jnp.stack([out1, out2], axis=-1).reshape(x.shape)
        key = jax.random.key(seed)
        k1, k2, k3 = jax.random.split(key, 3)
        batch, seq_len, embed_dim = (2, 256, 128)
        x = jax.random.normal(k1, (batch, seq_len, embed_dim), dtype=jnp.float32)
        W_qkv = jax.random.normal(k2, (embed_dim, 3 * NUM_HEADS * HEAD_DIM), dtype=jnp.float32) * 0.02
        W_out = jax.random.normal(k3, (NUM_HEADS * HEAD_DIM, embed_dim), dtype=jnp.float32) * 0.02
        return {'x': x, 'W_qkv': W_qkv, 'W_out': W_out}
    _L0_attn_in = _L0_attn_setup()

    def _L0_ffn_setup():
        import jax, jax.numpy as jnp
        import numpy as np
        B, S, H, F, E, TOPK = (4, 256, 128, 512, 8, 2)
        key = jax.random.key(seed)
        k0, k1, k2, k3, k4 = jax.random.split(key, 5)
        scale = 0.02
        return {'hidden_states': jax.random.normal(k0, (B, S, H), dtype=jnp.float32), 'router_w': jax.random.normal(k1, (E, H), dtype=jnp.float32) * scale, 'gate_w': jax.random.normal(k2, (E, F, H), dtype=jnp.float32) * scale, 'up_w': jax.random.normal(k3, (E, F, H), dtype=jnp.float32) * scale, 'down_w': jax.random.normal(k4, (E, H, F), dtype=jnp.float32) * scale}
    _L0_ffn_in = _L0_ffn_setup()
    _d = {'L0_attn_x': _L0_attn_in['x'], 'L0_attn_W_qkv': _L0_attn_in['W_qkv'], 'L0_attn_W_out': _L0_attn_in['W_out'], 'L0_ffn_router_w': _L0_ffn_in['router_w'], 'L0_ffn_gate_w': _L0_ffn_in['gate_w'], 'L0_ffn_up_w': _L0_ffn_in['up_w'], 'L0_ffn_down_w': _L0_ffn_in['down_w']}
    _x0 = _d['L0_attn_x']
    _d['L0_attn_x'] = jax.random.normal(jax.random.fold_in(jax.random.key(seed), 1), (8, 512, 128), dtype=_x0.dtype)
    del _x0
    return _d

def reference(L0_attn_x, L0_attn_W_qkv, L0_attn_W_out, L0_ffn_router_w, L0_ffn_gate_w, L0_ffn_up_w, L0_ffn_down_w):

    def _L0_attn_ref(x, W_qkv, W_out):
        import jax, jax.numpy as jnp
        import numpy as np
        NUM_HEADS = 16
        HEAD_DIM = 64
        NEG_INF = -1000000000.0

        def rotary_embedding(x, seq_len, head_dim):
            positions = jnp.arange(seq_len)
            dim_pairs = jnp.arange(0, head_dim, 2)
            freqs = 1.0 / 10000.0 ** (dim_pairs / head_dim)
            angles = positions[:, None] * freqs[None, :]
            cos = jnp.cos(angles)[:, None, :]
            sin = jnp.sin(angles)[:, None, :]
            x1 = x[..., ::2]
            x2 = x[..., 1::2]
            out1 = x1 * cos - x2 * sin
            out2 = x1 * sin + x2 * cos
            return jnp.stack([out1, out2], axis=-1).reshape(x.shape)
        batch, seq_len, embed_dim = x.shape
        qkv = jnp.einsum('bse,ef->bsf', x, W_qkv)
        qkv = qkv.reshape(batch, seq_len, 3, NUM_HEADS, HEAD_DIM)
        q, k, v = (qkv[:, :, 0], qkv[:, :, 1], qkv[:, :, 2])
        q = rotary_embedding(q, seq_len, HEAD_DIM)
        k = rotary_embedding(k, seq_len, HEAD_DIM)
        scale = 1.0 / jnp.sqrt(jnp.asarray(HEAD_DIM, dtype=x.dtype))
        scores = jnp.einsum('bqhd,bkhd->bhqk', q, k) * scale
        mask = jnp.tril(jnp.ones((seq_len, seq_len), dtype=bool))[None, None, :, :]
        scores = jnp.where(mask, scores, NEG_INF)
        weights = jax.nn.softmax(scores, axis=-1)
        out = jnp.einsum('bhqk,bkhd->bqhd', weights, v)
        out = out.reshape(batch, seq_len, NUM_HEADS * HEAD_DIM)
        return jnp.einsum('bsf,fe->bse', out, W_out)

    def _L0_ffn_ref(hidden_states, router_w, gate_w, up_w, down_w):
        import jax, jax.numpy as jnp
        import numpy as np
        B, S, H, F, E, TOPK = (4, 256, 128, 512, 8, 2)
        b, s, h = hidden_states.shape
        x = hidden_states.reshape(-1, h)
        router_logits = x @ router_w.T
        top_vals, top_idx = jax.lax.top_k(router_logits, TOPK)
        routing_weights = jax.nn.softmax(top_vals, axis=-1)
        combine = jnp.sum(jax.nn.one_hot(top_idx, E, dtype=x.dtype) * routing_weights[..., None], axis=1)
        out = jnp.zeros_like(x)
        for e in range(E):
            g = x @ gate_w[e].T
            u = x @ up_w[e].T
            y = jax.nn.silu(g) * u @ down_w[e].T
            out = out + combine[:, e:e + 1] * y
        return out.reshape(b, s, h)
    x = L0_attn_x
    x = x + 0.5 * _L0_ffn_ref(_layernorm(x, axis=-1), L0_ffn_router_w, L0_ffn_gate_w, L0_ffn_up_w, L0_ffn_down_w)
    x = x + _L0_attn_ref(_layernorm(x, axis=-1), L0_attn_W_qkv, L0_attn_W_out)
    x = x + 0.5 * _L0_ffn_ref(_layernorm(x, axis=-1), L0_ffn_router_w, L0_ffn_gate_w, L0_ffn_up_w, L0_ffn_down_w)
    return x

_drawn_inputs = setup_inputs


def setup_inputs(seed=0):
    import zlib

    import numpy as np

    out = dict(_drawn_inputs(seed))
    spreads = {}
    factors = {'L0_attn_W_qkv': 3.431,
     'L0_attn_W_out': 3.473,
     'L0_ffn_router_w': 7.799,
     'L0_ffn_gate_w': 6.809,
     'L0_ffn_up_w': 6.772,
     'L0_ffn_down_w': 6.771}
    for name, (base, spread) in spreads.items():
        noise = np.random.default_rng([zlib.crc32(name.encode()), seed]).standard_normal(out[name].shape)
        drawn = base * np.exp(spread * noise) if base else spread * noise
        out[name] = jnp.asarray(drawn.astype(out[name].dtype))
    for name, factor in factors.items():
        out[name] = (out[name] * factor).astype(out[name].dtype)
    return out
```

```python
from contextlib import ExitStack

import numpy as np

import concourse.bass as bass
from concourse import mybir

F32 = mybir.dt.float32
F32R = mybir.dt.float32r
BF16 = mybir.dt.bfloat16
ALU = mybir.AluOpType
ACT = mybir.ActivationFunctionType
AX = mybir.AxisListType.X

P = 128
HEADS = 16
HEAD_DIM = 64
PAIRS = HEADS // 2
MASKED = -1.0e30
EPS = 1e-5


def wait(eng, sem, value):
    if isinstance(value, int) and value <= 0:
        return
    eng.wait_ge(sem, value)


class Chain:

    def __init__(self, eng, sem):
        self.eng, self.sem, self.count = eng, sem, 0

    def __call__(self, instruction):
        self.count += 1
        instruction.then_inc(self.sem, 1)
        self.eng.wait_ge(self.sem, self.count)


def macaron(nc, x, w_qkv, w_out, router_t, gate_t, up_t, down_t, cos_t, sin_t, out):
    tokens, D = x.shape
    NB = tokens // P
    GROUPS = NB // 4
    SB = cos_t.shape[1]
    E = router_t.shape[1]
    FC = gate_t.shape[2] // P
    assert D == P and SB == 4

    with ExitStack() as top:
        def sb(name, shape, dt=F32, ctx=top):
            return ctx.enter_context(nc.sbuf_tensor(name, shape, dt))

        def sem(name):
            return top.enter_context(nc.semaphore(name))

        X = sb("X", [P, NB, D])
        ident = sb("ident", [P, P])
        identb = sb("identb", [P, P], BF16)
        causal = sb("causal", [P, P], BF16)
        stats = sb("stats", [P, NB, 6])
        mean = sb("mean", [P, NB])
        rstd = sb("rstd", [P, NB])
        tmpa = sb("tmpa", [P, NB])
        tmpb = sb("tmpb", [P, NB])

        loaded = sem("loaded")
        consts = sem("consts")
        with nc.Block() as block:
            @block.sync
            def _(sp):
                sp.dma_start(X[:, :, :], x.rearrange("(n p) d -> p n d", p=P)).then_inc(loaded, 16)
                sp.wait_ge(loaded, 16)

            @block.gpsimd
            def _(pool):
                pool.memset(ident[:, :], 0.0).then_inc(consts, 1)
                pool.memset(identb[:, :], 0.0).then_inc(consts, 1)
                pool.memset(causal[:, :], 0.0).then_inc(consts, 1)
                pool.wait_ge(consts, 3)
                for one in (ident, identb):
                    pool.affine_select(out=one[:, :], in_=one[:, :], compare_op=ALU.not_equal, fill=1.0,
                                       base=0, pattern=[[-1, P]], channel_multiplier=1).then_inc(consts, 1)
                pool.affine_select(out=causal[:, :], in_=causal[:, :], compare_op=ALU.is_ge, fill=MASKED,
                                   base=0, pattern=[[-1, P]], channel_multiplier=1).then_inc(consts, 1)
                pool.wait_ge(consts, 6)

        ffn(nc, "f1", X, gate_t, up_t, down_t, router_t, ident, stats, mean, rstd, tmpa, tmpb, NB, E, FC)
        attention(nc, X, w_qkv, w_out, cos_t, sin_t, ident, identb, causal,
                  stats, mean, rstd, tmpa, tmpb, NB)
        ffn(nc, "f2", X, gate_t, up_t, down_t, router_t, ident, stats, mean, rstd, tmpa, tmpb, NB, E, FC)

        stored = sem("stored")
        with nc.Block() as block:
            @block.sync
            def _(sp):
                sp.dma_start(out.rearrange("(n p) d -> p n d", p=P), X[:, :, :]).then_inc(stored, 16)
                sp.wait_ge(stored, 16)


def layernorm_stats(nc, name, ctx, X, stats, mean, rstd, tmpa, tmpb, NB):
    chain_sem = ctx.enter_context(nc.semaphore(name + "_stat_chain"))
    var_ready = ctx.enter_context(nc.semaphore(name + "_var_ready"))
    std_ready = ctx.enter_context(nc.semaphore(name + "_std_ready"))
    with nc.Block() as block:
        @block.vector
        def _(dve):
            link = Chain(dve, chain_sem)
            with dve.Fori(0, NB) as n:
                dve.bn_stats(stats[:, bass.ds(n, 1), :].rearrange("p a s -> p (a s)"),
                             X[:, bass.ds(n, 1), :].rearrange("p a d -> p (a d)")).then_inc(var_ready, 1)
            dve.wait_ge(var_ready, NB)
            me, mo = stats[:, :, 1], stats[:, :, 4]
            link(dve.tensor_tensor(tmpa[:, :], me, mo, ALU.subtract))
            link(dve.tensor_tensor(mean[:, :], me, mo, ALU.add))
            link(dve.tensor_tensor(tmpb[:, :], stats[:, :, 2], stats[:, :, 5], ALU.add))
            link(dve.tensor_tensor(tmpa[:, :], tmpa[:, :], tmpa[:, :], ALU.mult))
            link(dve.tensor_scalar(mean[:, :], mean[:, :], 0.5, None, ALU.mult))
            link(dve.tensor_scalar(tmpb[:, :], tmpb[:, :], 1.0 / P, EPS, ALU.mult, ALU.add))
            dve.scalar_tensor_tensor(out=tmpa[:, :], in0=tmpa[:, :], scalar=0.25, in1=tmpb[:, :],
                                     op0=ALU.mult, op1=ALU.add).then_inc(var_ready, 1)
            dve.wait_ge(std_ready, 1)
            link(dve.reciprocal(rstd[:, :], tmpb[:, :]))
            link(dve.tensor_tensor(tmpb[:, :], rstd[:, :], rstd[:, :], ALU.mult))
            link(dve.tensor_tensor(tmpb[:, :], tmpb[:, :], tmpa[:, :], ALU.mult))
            link(dve.tensor_scalar(tmpb[:, :], tmpb[:, :], -0.5, 1.5, ALU.mult, ALU.add))
            link(dve.tensor_tensor(rstd[:, :], rstd[:, :], tmpb[:, :], ALU.mult))

        @block.scalar
        def _(act):
            act.wait_ge(var_ready, NB + 1)
            act.activation(tmpb[:, :], tmpa[:, :], ACT.Sqrt).then_inc(std_ready, 1)


def ffn(nc, name, X, gate_t, up_t, down_t, router_t, ident, stats, mean, rstd, tmpa, tmpb, NB, E, FC):
    GROUPS = NB // 4
    F = FC * P
    with ExitStack() as ctx:
        def sb(n, shape, dt=F32):
            return ctx.enter_context(nc.sbuf_tensor(f"{name}_{n}", shape, dt))

        def ps(n):
            return ctx.enter_context(nc.psum_tensor(f"{name}_{n}", [P, 512], F32))

        def sem(n):
            return ctx.enter_context(nc.semaphore(f"{name}_{n}"))

        layernorm_stats(nc, name, ctx, X, stats, mean, rstd, tmpa, tmpb, NB)

        XT = sb("XT", [P, NB * P])
        gate = sb("gate", [P, E, F])
        up = sb("up", [P, E, F])
        down = sb("down", [P, E, FC, P])
        router = sb("router", [P, E])
        xn = [sb(f"xn{k}", [P, 4, P]) for k in range(2)]
        xts = [sb(f"xts{k}", [P, 512]) for k in range(2)]
        logits = sb("logits", [P, NB, E])
        comb = sb("comb", [P, NB, E])
        top8 = sb("top8", [P, NB, 8])
        idx8 = sb("idx8", [P, 8 * NB], mybir.dt.uint32)
        idxf = sb("idxf", [P, 8 * NB])
        iota = sb("iota", [P, E])
        iotai = sb("iotai", [P, E], mybir.dt.int32)
        wts = sb("wts", [P, 4, NB])
        oh = sb("oh", [P, 2, NB, E])
        silu = [sb(f"silu{k}", [P, 512]) for k in range(2)]
        hid = [sb(f"hid{k}", [P, FC, 512]) for k in range(2)]
        bank = [ps(f"b{k}") for k in range(8)]

        w_in = sem("w_in")
        iota_ready = sem("iota_ready")
        xn_ready = sem("xn_ready")
        xt_psum = sem("xt_psum")
        xts_ready = sem("xts_ready")
        xt_ready = sem("xt_ready")
        lg_psum = sem("lg_psum")
        lg_ready = sem("lg_ready")
        with nc.Block() as block:
            @block.sync
            def _(sp):
                sp.dma_start(router[:, :], router_t).then_inc(w_in, 16)
                sp.dma_start(gate[:, :, :], gate_t).then_inc(w_in, 16)
                sp.dma_start(up[:, :, :], up_t).then_inc(w_in, 16)
                sp.dma_start(down[:, :, :, :], down_t).then_inc(w_in, 16)
                sp.wait_ge(w_in, 64)

            @block.gpsimd
            def _(pool):
                pool.iota(iotai[:, :], pattern=[[1, E]], base=0, channel_multiplier=0).then_inc(iota_ready, 1)
                pool.wait_ge(iota_ready, 1)
                pool.tensor_copy(iota[:, :], iotai[:, :]).then_inc(iota_ready, 1)
                pool.wait_ge(iota_ready, 2)

            def xt_keep(dve, g, k):
                dve.wait_ge(xts_ready, g + 1)
                dve.tensor_copy(XT[:, bass.ds(g * 512, 512)], bank[k][:, :]).then_inc(xt_ready, 1)
                dve.wait_ge(lg_psum, g + 1)
                dve.tensor_copy(logits[:, bass.ds(g * 4, 4), :],
                                bank[2 + k][:, 0:4 * E].rearrange("p (t e) -> p t e", t=4)).then_inc(lg_ready, 1)

            @block.vector
            def _(dve):
                with dve.Fori(0, GROUPS // 2) as gg:
                    for k in range(2):
                        g = gg * 2 + k
                        for t in range(4):
                            n = g * 4 + t
                            one = dve.tensor_scalar(xn[k][:, t, :], X[:, bass.ds(n, 1), :].rearrange("p a d -> p (a d)"),
                                                    mean[:, bass.ds(n, 1)], rstd[:, bass.ds(n, 1)],
                                                    ALU.subtract, ALU.mult)
                        one.then_inc(xn_ready, 1)
                        xt_keep(dve, g, k)

            @block.scalar
            def _(act):
                with act.Fori(0, GROUPS // 2) as gg:
                    for k in range(2):
                        g = gg * 2 + k
                        act.wait_ge(xt_psum, g + 1)
                        act.activation(xts[k][:, :], bank[k][:, :], ACT.Copy).then_inc(xts_ready, 1)

            @block.tensor
            def _(pe):
                pe.wait_ge(w_in, 64)
                with pe.Fori(0, GROUPS // 2) as gg:
                    for k in range(2):
                        g = gg * 2 + k
                        pe.wait_ge(xn_ready, g + 1)
                        for t in range(4):
                            one = pe.transpose(bank[k][:, t * P:(t + 1) * P], xn[k][:, t, :], ident[:, :])
                        one.then_inc(xt_psum, 1)
                        pe.wait_ge(xts_ready, g + 1)
                        for t in range(4):
                            one = pe.matmul(bank[2 + k][:, t * E:(t + 1) * E], xts[k][:, t * P:(t + 1) * P],
                                            router[:, :], start=True, stop=True)
                        one.then_inc(lg_psum, 1)

        rc = sem("rc")
        ex_in = sem("ex_in")
        ex_out = sem("ex_out")
        mxd = sem("mxd")
        with nc.Block() as block:
            @block.vector
            def _(dve):
                link = Chain(dve, rc)
                for n in range(NB):
                    dve.max(top8[:, n, :], logits[:, n, :]).then_inc(mxd, 1)
                dve.wait_ge(mxd, NB)
                for n in range(NB):
                    dve.max_index(idx8[:, 8 * n:8 * n + 8], top8[:, n, :], logits[:, n, :]).then_inc(mxd, 1)
                dve.wait_ge(mxd, 2 * NB)
                link(dve.tensor_copy(idxf[:, :], idx8[:, :]))
                dve.tensor_tensor(wts[:, 0, :], top8[:, :, 1], top8[:, :, 0], ALU.subtract).then_inc(ex_in, 1)
                dve.wait_ge(ex_out, 1)
                link(dve.tensor_scalar(wts[:, 2, :], wts[:, 1, :], 1.0, None, ALU.add))
                link(dve.reciprocal(wts[:, 2, :], wts[:, 2, :]))
                link(dve.tensor_scalar(wts[:, 2, :], wts[:, 2, :], 0.5, None, ALU.mult))
                link(dve.tensor_tensor(wts[:, 3, :], wts[:, 2, :], wts[:, 1, :], ALU.mult))
                iv = idxf[:, :].rearrange("p (n k) -> p n k", k=8)
                for k in range(2):
                    link(dve.tensor_tensor(oh[:, k, :, :], iv[:, :, k:k + 1].to_broadcast([P, NB, E]),
                                           iota[:, :].rearrange("p (a e) -> p a e", a=1).to_broadcast([P, NB, E]),
                                           ALU.is_equal))
                    link(dve.tensor_tensor(oh[:, k, :, :], oh[:, k, :, :],
                                           wts[:, 2 + k, :].rearrange("p (n a) -> p n a", a=1).to_broadcast([P, NB, E]),
                                           ALU.mult))
                link(dve.tensor_tensor(comb[:, :, :], oh[:, 0, :, :], oh[:, 1, :, :], ALU.add))

            @block.scalar
            def _(act):
                act.wait_ge(ex_in, 1)
                act.activation(wts[:, 1, :], wts[:, 0, :], ACT.Exp).then_inc(ex_out, 1)

        STEPS = E * FC
        gu_psum = sem("gu_psum")
        silu_ready = sem("silu_ready")
        hid_ready = sem("hid_ready")
        y_psum = sem("y_psum")
        y_used = sem("y_used")
        GB, UB, YB = bank[0:2], bank[2:4], bank[4:6]
        with nc.Block() as block:
            @block.tensor
            def _(pe):
                with pe.Fori(0, GROUPS) as g:
                    def down_proj(e):
                        n = g * E + e
                        pe.wait_ge(hid_ready, g * STEPS + (e + 1) * FC)
                        if e >= 2:
                            pe.wait_ge(y_used, n - 1)
                        for t in range(4):
                            for c in range(FC):
                                one = pe.matmul(YB[e % 2][:, t * P:(t + 1) * P], hid[e % 2][:, c, t * P:(t + 1) * P],
                                                down[:, e, c, :], start=(c == 0), stop=(c == FC - 1))
                        one.then_inc(y_psum, 1)

                    for s in range(STEPS):
                        e, c = divmod(s, FC)
                        n = g * STEPS + s
                        if s >= 2:
                            pe.wait_ge(hid_ready, n - 1)
                        rhs = XT[:, bass.ds(g * 512, 512)]
                        pe.matmul(GB[s % 2][:, :], gate[:, e, c * P:(c + 1) * P], rhs, start=True, stop=True)
                        pe.matmul(UB[s % 2][:, :], up[:, e, c * P:(c + 1) * P], rhs, start=True,
                                  stop=True).then_inc(gu_psum, 1)
                        if c == 1 and e >= 1:
                            down_proj(e - 1)
                    down_proj(E - 1)
                    pe.wait_ge(y_used, g * E + E)

            @block.scalar
            def _(act):
                with act.Fori(0, GROUPS) as g:
                    for s in range(STEPS):
                        n = g * STEPS + s
                        act.wait_ge(gu_psum, n + 1)
                        if s >= 2:
                            act.wait_ge(hid_ready, n - 1)
                        act.activation(silu[s % 2][:, :], GB[s % 2][:, :], ACT.Silu).then_inc(silu_ready, 1)

            @block.vector
            def _(dve):
                with dve.Fori(0, GROUPS) as g:
                    def add(e):
                        n = g * E + e
                        dve.wait_ge(y_psum, n + 1)
                        if e >= 1:
                            dve.wait_ge(y_used, n)
                        for t in range(4):
                            tok = X[:, bass.ds(g * 4 + t, 1), :].rearrange("p a d -> p (a d)")
                            cw = comb[:, bass.ds(g * 4 + t, 1), e]
                            one = dve.scalar_tensor_tensor(out=tok, in0=YB[e % 2][:, t * P:(t + 1) * P], scalar=cw,
                                                           in1=tok, op0=ALU.mult, op1=ALU.add)
                        one.then_inc(y_used, 1)

                    for s in range(STEPS):
                        e, c = divmod(s, FC)
                        n = g * STEPS + s
                        dve.wait_ge(silu_ready, n + 1)
                        if c == 0 and e >= 2:
                            dve.wait_ge(y_psum, g * E + e - 1)
                        dve.tensor_tensor(hid[e % 2][:, c, :], UB[s % 2][:, :], silu[s % 2][:, :],
                                          ALU.mult).then_inc(hid_ready, 1)
                        if c == 3 and e >= 1:
                            add(e - 1)
                    add(E - 1)


def attention(nc, X, w_qkv, w_out, cos_t, sin_t, ident, identb, causal, stats, mean, rstd, tmpa, tmpb, NB):
    SCALE = HEAD_DIM ** -0.5
    GROUPS = NB // 4
    STEPS = GROUPS * PAIRS
    QKV = 3 * P
    with ExitStack() as ctx:
        def sb(n, shape, dt=F32):
            return ctx.enter_context(nc.sbuf_tensor("at_" + n, shape, dt))

        def ps(n):
            return ctx.enter_context(nc.psum_tensor("at_" + n, [P, 512], F32))

        def sem(n):
            return ctx.enter_context(nc.semaphore("at_" + n))

        layernorm_stats(nc, "at", ctx, X, stats, mean, rstd, tmpa, tmpb, NB)

        XT = sb("XT", [P, 2, NB * P], F32R)
        w_hi = sb("w_hi", [P, PAIRS, QKV], F32R)
        w_lo = sb("w_lo", [P, PAIRS, QKV], F32R)
        wo = sb("wo", [P, PAIRS, P])
        cos = sb("cos", [P, 4, HEAD_DIM])
        sin = sb("sin", [P, 4, HEAD_DIM])
        bank = [ps(f"b{k}") for k in range(8)]

        w_in = sem("w_in")
        w_his = sem("w_his")
        w_los = sem("w_los")
        xn_ready = sem("xn_ready")
        xt_psum = sem("xt_psum")
        hi_ready = sem("hi_ready")
        lo_ready = sem("lo_ready")

        with ExitStack() as early:
            w_all = early.enter_context(nc.sbuf_tensor("at_w_all", [P, PAIRS, QKV], F32))
            xn = [early.enter_context(nc.sbuf_tensor(f"at_xn{k}", [P, 4, P], F32)) for k in range(2)]
            with nc.Block() as block:
                @block.sync
                def _(sp):
                    w_v = w_qkv.rearrange("e (t j c) -> e t j c", t=3, j=PAIRS)
                    for t in range(3):
                        sp.dma_start(w_all[:, :, t * P:(t + 1) * P], w_v[:, t, :, :]).then_inc(w_in, 16)
                    sp.dma_start(wo[:, :, :], w_out.rearrange("(j f) e -> f j e", f=P)).then_inc(w_in, 16)
                    sp.dma_start(cos[:, :, :], cos_t).then_inc(w_in, 16)
                    sp.dma_start(sin[:, :, :], sin_t).then_inc(w_in, 16)
                    sp.wait_ge(w_in, 96)

                @block.gpsimd
                def _(pool):
                    for j in range(PAIRS):
                        pool.wait_ge(w_his, j + 1)
                        pool.tensor_tensor(w_lo[:, j, :], w_all[:, j, :], w_hi[:, j, :].bitcast(F32),
                                           ALU.subtract).then_inc(w_los, 1)
                    pool.wait_ge(w_los, PAIRS)

                @block.vector
                def _(dve):
                    with dve.Fori(0, GROUPS // 2) as gg:
                        for k in range(2):
                            g = gg * 2 + k
                            for t in range(4):
                                n = g * 4 + t
                                one = dve.tensor_scalar(xn[k][:, t, :],
                                                        X[:, bass.ds(n, 1), :].rearrange("p a d -> p (a d)"),
                                                        mean[:, bass.ds(n, 1)], rstd[:, bass.ds(n, 1)],
                                                        ALU.subtract, ALU.mult)
                            one.then_inc(xn_ready, 1)
                            dve.wait_ge(hi_ready, g + 1)
                            cols = bass.ds(g * 512, 512)
                            dve.tensor_tensor(XT[:, 1, cols], bank[k][:, :], XT[:, 0, cols].bitcast(F32),
                                              ALU.subtract).then_inc(lo_ready, 1)

                @block.scalar
                def _(act):
                    act.wait_ge(w_in, 96)
                    for j in range(PAIRS):
                        act.activation(w_hi[:, j, :], w_all[:, j, :], ACT.Copy).then_inc(w_his, 1)
                    with act.Fori(0, GROUPS // 2) as gg:
                        for k in range(2):
                            g = gg * 2 + k
                            act.wait_ge(xt_psum, g + 1)
                            act.activation(XT[:, 0, bass.ds(g * 512, 512)], bank[k][:, :],
                                           ACT.Copy).then_inc(hi_ready, 1)

                @block.tensor
                def _(pe):
                    with pe.Fori(0, GROUPS // 2) as gg:
                        for k in range(2):
                            g = gg * 2 + k
                            pe.wait_ge(xn_ready, g + 1)
                            for t in range(4):
                                one = pe.transpose(bank[k][:, t * P:(t + 1) * P], xn[k][:, t, :], ident[:, :])
                            one.then_inc(xt_psum, 1)

        xs = sb("xs", [P, 2, 512], F32R)
        ra = [sb(f"ra{k}", [P, 4, HEAD_DIM]) for k in range(2)]
        rb = [sb(f"rb{k}", [P, 4, HEAD_DIM]) for k in range(2)]
        R = sb("R", [P, 4, 2, P])
        QT = [sb(f"QT{k}", [P, 512]) for k in range(2)]
        KT = [[sb(f"KT{k}{h}", [P, 512]) for h in range(2)] for k in range(2)]
        v_new = sb("v_new", [P, 4, P])
        V = [sb(f"V{k}", [P, 4, P]) for k in range(2)]
        prob = [sb(f"prob{k}", [P, 512]) for k in range(4)]
        probT = [sb(f"probT{k}", [P, 4, P]) for k in range(4)]
        OT = sb("OT", [P, 512])
        mx = sb("mx", [P, 4])
        nb = sb("nb", [P, 4])
        sums = sb("sums", [P, 4])
        rec = sb("rec", [P, 4])
        qkv_bank, s_bank, pt_bank = bank[0:2], bank[2:4], bank[4:6]
        o_bank, misc = bank[6], bank[7]

        kt_zero = sem("kt_zero")
        xs_in = sem("xs_in")
        qkv_psum = sem("qkv_psum")
        rope_ready = sem("rope_ready")
        v_ready = sem("v_ready")
        v_moved = sem("v_moved")
        r_ready = sem("r_ready")
        qt_psum = sem("qt_psum")
        kt_psum = sem("kt_psum")
        qt_ready = sem("qt_ready")
        kt_ready = sem("kt_ready")
        s_psum = sem("s_psum")
        mx_ready = sem("mx_ready")
        nb_ready = sem("nb_ready")
        exp_ready = sem("exp_ready")
        rec_ready = sem("rec_ready")
        prob_ready = sem("prob_ready")
        pt_psum = sem("pt_psum")
        ptA_ready = sem("ptA_ready")
        ptB_ready = sem("ptB_ready")
        pv_psum = sem("pv_psum")
        ot_ready = sem("ot_ready")
        y_psum = sem("y_psum")
        y_used = sem("y_used")
        pt_ready = (ptA_ready, ptB_ready)

        def program(eng, step):
            for i in (-1, 0, 1):
                step(eng, i, i % 2)
            with eng.Fori(0, (STEPS - 4) // 2) as k:
                step(eng, k * 2 + 2, 0)
                step(eng, k * 2 + 3, 1)
            for i in (STEPS - 2, STEPS - 1, STEPS):
                step(eng, i, i % 2)

        def has(i, j):
            return not isinstance(i, int) or 0 <= i + j < STEPS

        with nc.Block() as block:
            @block.sync
            def _(sp):
                def step(sp, i, kk):
                    if has(i, 1):
                        wait(sp, qkv_psum, 4 * i + 4)
                        g = (i + 1) // PAIRS
                        sp.dma_start(xs[:, :, :].bitcast(F32),
                                     XT[:, :, bass.ds(g * 512, 512)].bitcast(F32)).then_inc(xs_in, 16)
                        sp.wait_ge(v_ready, 4 * i + 8)
                        wait(sp, pv_psum, 4 * i)
                        sp.dma_start(V[1 - kk][:, :, :], v_new[:, :, :]).then_inc(v_moved, 16)
                program(sp, step)
                sp.wait_ge(xs_in, 16 * STEPS)
                sp.wait_ge(v_moved, 16 * STEPS)

            @block.gpsimd
            def _(pool):
                for k in range(2):
                    pool.memset(KT[k][0][64:128, :], 0.0).then_inc(kt_zero, 1)
                    pool.memset(KT[k][1][0:64, :], 0.0).then_inc(kt_zero, 1)

                def step(pool, i, kk):
                    if has(i, 1):
                        wait(pool, kt_psum, i + 1)
                        for t in range(4):
                            pool.wait_ge(rope_ready, 4 * (i + 1) + t + 1)
                            o = R[:, t, :, :].rearrange("p a (c two) -> p (a c) two", two=2)
                            a = ra[t % 2][:, :, :].rearrange("p h (c two) -> p (h c) two", two=2)
                            b = rb[t % 2][:, :, :].rearrange("p h (c two) -> p (h c) two", two=2)
                            for z in range(2):
                                one = pool.tensor_tensor(o[:, :, z], a[:, :, z], b[:, :, 1 - z], ALU.add)
                            one.then_inc(r_ready, 1)
                program(pool, step)

            @block.tensor
            def _(pe):
                def project(i, t):
                    if t == 0:
                        pe.wait_ge(xs_in, 16 * i + 16)
                    wait(pe, v_ready, 4 * i + t - 1)
                    j = i % PAIRS
                    hi, lo = xs[:, 0, t * P:(t + 1) * P], xs[:, 1, t * P:(t + 1) * P]
                    wh = w_hi[:, bass.ds(j, 1), :].rearrange("p a c -> p (a c)")
                    wl = w_lo[:, bass.ds(j, 1), :].rearrange("p a c -> p (a c)")
                    o = qkv_bank[t % 2][:, 0:QKV]
                    pe.matmul(o, hi, wh, start=True, stop=False)
                    pe.matmul(o, hi, wl, start=False, stop=False)
                    pe.matmul(o, lo, wh, start=False, stop=True).then_inc(qkv_psum, 1)

                def turn(i, which):
                    if which == 0:
                        pe.wait_ge(r_ready, 4 * i + 4)
                        wait(pe, y_used, i - 2)
                    else:
                        pe.wait_ge(qt_ready, i + 1)
                    for t in range(4):
                        one = pe.transpose(misc[:, t * P:(t + 1) * P], R[:, t, which, :], ident[:, :])
                    one.then_inc((qt_psum, kt_psum)[which], 1)

                def scores(i, kk, u):
                    qb, h = divmod(u, 2)
                    U = 8 * i + u
                    if u == 0:
                        pe.wait_ge(kt_ready, i + 1)
                    wait(pe, exp_ready, U - 1)
                    n = (qb + 1) * P
                    pe.matmul(s_bank[h][:, 0:n], QT[kk][:, qb * P:n], KT[kk][h][:, 0:n], start=True, stop=False)
                    pe.matmul(s_bank[h][:, qb * P:n], identb[:, :], causal[:, :], start=False,
                              stop=True).then_inc(s_psum, 1)

                def turn_probs(i, u):
                    qb, h = divmod(u, 2)
                    U = 8 * i + u
                    pe.wait_ge(prob_ready, U + 1)
                    wait(pe, pt_ready[h], 4 * i + qb)
                    for b in range(qb + 1):
                        one = pe.transpose(pt_bank[h][:, b * P:(b + 1) * P], prob[u % 4][:, b * P:(b + 1) * P],
                                           ident[:, :])
                    one.then_inc(pt_psum, 1)

                def weigh(i, kk, qb):
                    if qb == 0:
                        pe.wait_ge(v_moved, 16 * i + 16)
                        wait(pe, ot_ready, i)
                    pe.wait_ge(ptA_ready, 4 * i + qb + 1)
                    pe.wait_ge(ptB_ready, 4 * i + qb + 1)
                    for b in range(qb + 1):
                        for h in range(2):
                            one = pe.matmul(o_bank[64 * h:64 * h + 64, qb * P:(qb + 1) * P],
                                            V[kk][:, b, 64 * h:64 * h + 64],
                                            probT[(2 * qb + h) % 4][:, b, :], start=(b == 0), stop=(b == qb))
                    one.then_inc(pv_psum, 1)

                def out_project(i, last):
                    pe.wait_ge(ot_ready, i + 1)
                    if last:
                        wait(pe, y_used, i)
                    else:
                        pe.wait_ge(kt_ready, i + 3)
                    j = i % PAIRS
                    for t in range(4):
                        one = pe.matmul(misc[:, t * P:(t + 1) * P], OT[:, t * P:(t + 1) * P],
                                        wo[:, bass.ds(j, 1), :].rearrange("p a c -> p (a c)"),
                                        start=True, stop=True)
                    one.then_inc(y_psum, 1)

                def step(pe, i, kk):
                    for u in range(8):
                        if has(i, 0):
                            scores(i, kk, u)
                        if has(i, 1) and u < 4:
                            project(i + 1, u)
                        if has(i, 1) and u in (5, 6):
                            turn(i + 1, u - 5)
                        if u == 7 and has(i, -1):
                            out_project(i - 1, not has(i, 1))
                        if u < 3 and has(i, -1):
                            turn_probs(i - 1, u + 5)
                        if u >= 3 and has(i, 0):
                            turn_probs(i, u - 3)
                        if u in (0, 2, 4) and has(i, -1):
                            weigh(i - 1, 1 - kk, 1 + u // 2)
                        if u == 6 and has(i, 0):
                            weigh(i, kk, 0)
                pe.wait_ge(kt_zero, 4)
                program(pe, step)

            @block.vector
            def _(dve):
                def rope(i, t):
                    dve.wait_ge(qkv_psum, 4 * i + t + 1)
                    wait(dve, r_ready, 4 * i + t - 1)
                    qk = qkv_bank[t % 2][:, 0:4 * HEAD_DIM].rearrange("p (h c) -> p h c", h=4)
                    for dst, table in ((ra, cos), (rb, sin)):
                        one = dve.tensor_tensor(dst[t % 2][:, :, :], qk,
                                                table[:, t:t + 1, :].to_broadcast([P, 4, HEAD_DIM]), ALU.mult)
                    one.then_inc(rope_ready, 1)

                def maximum(i, u):
                    qb, h = divmod(u, 2)
                    U = 8 * i + u
                    c = u % 4
                    dve.wait_ge(s_psum, U + 1)
                    dve.reduce_max(mx[:, c:c + 1], s_bank[h][:, 0:(qb + 1) * P], AX).then_inc(mx_ready, 1)
                    dve.wait_ge(mx_ready, U + 1)
                    dve.tensor_scalar(nb[:, c:c + 1], mx[:, c:c + 1], -SCALE, None, ALU.mult).then_inc(nb_ready, 1)

                def normalise(i, u):
                    qb, h = divmod(u, 2)
                    U = 8 * i + u
                    c = u % 4
                    dve.wait_ge(exp_ready, U + 1)
                    dve.reciprocal(rec[:, c:c + 1], sums[:, c:c + 1]).then_inc(rec_ready, 1)
                    dve.wait_ge(rec_ready, U + 1)
                    w = prob[c][:, 0:(qb + 1) * P]
                    dve.tensor_scalar(w, w, rec[:, c:c + 1], None, ALU.mult).then_inc(prob_ready, 1)

                def copy_b(i, u):
                    qb, h = divmod(u, 2)
                    dve.wait_ge(pt_psum, 8 * i + u + 1)
                    wait(dve, pv_psum, 4 * i + qb - 1)
                    dve.tensor_copy(probT[u % 4][:, 0:qb + 1, :],
                                    pt_bank[h][:, 0:(qb + 1) * P].rearrange("p (b q) -> p b q", q=P)
                                    ).then_inc(ptB_ready, 1)

                def residual(i):
                    dve.wait_ge(y_psum, i + 1)
                    wait(dve, y_used, i)
                    tok = X[:, bass.ds((i // PAIRS) * 4, 4), :]
                    dve.tensor_tensor(tok, misc[:, :].rearrange("p (t d) -> p t d", t=4), tok,
                                      ALU.add).then_inc(y_used, 1)

                def step(dve, i, kk):
                    for u in range(8):
                        if has(i, 0):
                            maximum(i, u)
                        if has(i, 1) and u < 4:
                            rope(i + 1, u)
                        if u == 0 and has(i, -1):
                            normalise(i - 1, 7)
                        if u > 0 and has(i, 0):
                            normalise(i, u - 1)
                        if u in (1, 3) and has(i, -1):
                            copy_b(i - 1, u + 4)
                        if u in (5, 7) and has(i, 0):
                            copy_b(i, u - 4)
                        if u == 7 and has(i, -1):
                            residual(i - 1)
                program(dve, step)

            @block.scalar
            def _(act):
                def values(i, t):
                    act.wait_ge(rope_ready, 4 * i + t + 1)
                    if t == 0:
                        wait(act, v_moved, 16 * i)
                    act.activation(v_new[:, t, :], qkv_bank[t % 2][:, 2 * P:3 * P], ACT.Copy).then_inc(v_ready, 1)

                def exponent(i, u):
                    qb, h = divmod(u, 2)
                    U = 8 * i + u
                    c = u % 4
                    act.wait_ge(nb_ready, U + 1)
                    wait(act, pt_psum, U - 3)
                    n = (qb + 1) * P
                    act.activation(prob[c][:, 0:n], s_bank[h][:, 0:n], ACT.Exp, bias=nb[:, c:c + 1], scale=SCALE,
                                   accum_out=sums[:, c:c + 1]).then_inc(exp_ready, 1)

                def copy_a(i, u):
                    qb, h = divmod(u, 2)
                    act.wait_ge(pt_psum, 8 * i + u + 1)
                    wait(act, pv_psum, 4 * i + qb - 1)
                    act.activation(probT[u % 4][:, 0:qb + 1, :],
                                   pt_bank[h][:, 0:(qb + 1) * P].rearrange("p (b q) -> p b q", q=P),
                                   ACT.Copy).then_inc(ptA_ready, 1)

                def queries(i, kk):
                    act.wait_ge(qt_psum, i + 1)
                    wait(act, s_psum, 8 * (i - 1))
                    act.activation(QT[kk][:, :], misc[:, :], ACT.Copy).then_inc(qt_ready, 1)

                def keys(i, kk):
                    act.wait_ge(kt_psum, i + 1)
                    wait(act, s_psum, 8 * (i - 1))
                    act.activation(KT[kk][0][0:64, :], misc[0:64, :], ACT.Copy)
                    act.activation(KT[kk][1][64:128, :], misc[64:128, :], ACT.Copy).then_inc(kt_ready, 1)

                def outputs(i):
                    act.wait_ge(pv_psum, 4 * i + 4)
                    wait(act, y_psum, i)
                    act.activation(OT[:, :], o_bank[:, :], ACT.Copy).then_inc(ot_ready, 1)

                def step(act, i, kk):
                    for u in range(8):
                        if has(i, 1) and 1 <= u <= 4:
                            values(i + 1, u - 1)
                        if u in (0, 2) and has(i, -1):
                            copy_a(i - 1, u + 4)
                        if u in (4, 6) and has(i, 0):
                            copy_a(i, u - 4)
                        if u == 5 and has(i, -1):
                            outputs(i - 1)
                        if u == 6 and has(i, 1):
                            queries(i + 1, 1 - kk)
                        if u == 7 and has(i, 1):
                            keys(i + 1, 1 - kk)
                        if has(i, 0):
                            exponent(i, u)
                program(act, step)


def kernel(**inputs):
    import concourse.bacc as bacc
    from concourse.bass_utils import run_bass_kernel_spmd

    x = np.ascontiguousarray(inputs["L0_attn_x"])
    batch, seq, dim = x.shape
    half = np.arange(0, HEAD_DIM, 2)
    freqs = (np.float32(1.0) / np.float32(10000.0) ** (half / HEAD_DIM).astype(np.float32)).astype(np.float32)
    angles = (np.arange(seq).astype(np.float32)[:, None] * freqs[None, :]).astype(np.float32)
    cos = np.repeat(np.cos(angles), 2, axis=1).astype(np.float32)
    sin = np.repeat(np.sin(angles), 2, axis=1).astype(np.float32) * np.tile(np.float32([1, -1]), HEAD_DIM // 2)
    by_position = lambda t: np.ascontiguousarray(t.reshape(seq // P, P, HEAD_DIM).transpose(1, 0, 2))
    down = inputs["L0_ffn_down_w"]
    E, D, F = down.shape
    arrays = {
        "x": x.reshape(batch * seq, dim),
        "w_qkv": np.ascontiguousarray(inputs["L0_attn_W_qkv"]),
        "w_out": np.ascontiguousarray(inputs["L0_attn_W_out"]),
        "router_t": np.ascontiguousarray(inputs["L0_ffn_router_w"].T),
        "gate_t": np.ascontiguousarray(inputs["L0_ffn_gate_w"].transpose(2, 0, 1)),
        "up_t": np.ascontiguousarray(inputs["L0_ffn_up_w"].transpose(2, 0, 1)),
        "down_t": np.ascontiguousarray(down.reshape(E, D, F // P, P).transpose(3, 0, 2, 1)),
        "cos_t": by_position(cos),
        "sin_t": by_position(sin),
    }
    nc = bacc.Bacc("TRN2", target_bir_lowering=False, num_devices=1)
    args = [nc.dram_tensor(k, a.shape, mybir.dt.from_np(a.dtype), kind="ExternalInput").ap()
            for k, a in arrays.items()]
    out = nc.dram_tensor("out", (batch * seq, dim), F32, kind="ExternalOutput").ap()
    macaron(nc, *args, out)
    r = run_bass_kernel_spmd(nc, [arrays], core_ids=[0])
    return r.results[0]["out"].reshape(batch, seq, dim)
```

```python
from contextlib import ExitStack

import numpy as np

import concourse.bass as bass
from concourse import mybir

F32 = mybir.dt.float32
F32R = mybir.dt.float32r
BF16 = mybir.dt.bfloat16
I32 = mybir.dt.int32
U32 = mybir.dt.uint32
ALU = mybir.AluOpType
ACT = mybir.ActivationFunctionType
AX = mybir.AxisListType.X

P = 128
HEADS = 16
HEAD_DIM = 64
PAIRS = HEADS // 2
MASKED = -1.0e30
EPS = 1e-5


def wait(eng, sem, value):
    if isinstance(value, int) and value <= 0:
        return
    eng.wait_ge(sem, value)


class Chain:

    def __init__(self, eng, sem):
        self.eng, self.sem, self.count = eng, sem, 0

    def __call__(self, instruction):
        self.count += 1
        instruction.then_inc(self.sem, 1)
        self.eng.wait_ge(self.sem, self.count)


def macaron(nc, x, w_qkv, w_out, router_t, gate_t, up_t, down_t, cos_t, sin_t, out):
    tokens, D = x.shape
    NB = tokens // P
    GROUPS = NB // 4
    SB = cos_t.shape[1]
    E = router_t.shape[1]
    FC = gate_t.shape[2] // P
    assert D == P and SB == 4

    with ExitStack() as top:
        def sb(name, shape, dt=F32, ctx=top):
            return ctx.enter_context(nc.sbuf_tensor(name, shape, dt))

        def sem(name):
            return top.enter_context(nc.semaphore(name))

        X = sb("X", [P, NB, D])
        ident = sb("ident", [P, P])
        identb = sb("identb", [P, P], BF16)
        causal = sb("causal", [P, P], BF16)
        tri = sb("tri", [P, P])
        ones = sb("ones", [P, P])
        xn_dram = nc.dram_tensor("xn_dram", (tokens, D), F32).ap()
        ys_dram = nc.dram_tensor("ys_dram", (2 * tokens + (2 * NB + E) * P, D), F32).ap()
        stats = sb("stats", [P, NB, 6])
        mean = sb("mean", [P, NB])
        rstd = sb("rstd", [P, NB])
        tmpa = sb("tmpa", [P, NB])
        tmpb = sb("tmpb", [P, NB])

        loaded = sem("loaded")
        consts = sem("consts")
        with nc.Block() as block:
            @block.sync
            def _(sp):
                sp.dma_start(X[:, :, :], x.rearrange("(n p) d -> p n d", p=P)).then_inc(loaded, 16)
                sp.wait_ge(loaded, 16)

            @block.gpsimd
            def _(pool):
                pool.memset(ones[:, :], 1.0).then_inc(consts, 1)
                pool.memset(ident[:, :], 0.0).then_inc(consts, 1)
                pool.memset(identb[:, :], 0.0).then_inc(consts, 1)
                pool.memset(causal[:, :], 0.0).then_inc(consts, 1)
                pool.wait_ge(consts, 4)
                for one in (ident, identb):
                    pool.affine_select(out=one[:, :], in_=one[:, :], compare_op=ALU.not_equal, fill=1.0,
                                       base=0, pattern=[[-1, P]], channel_multiplier=1).then_inc(consts, 1)
                pool.affine_select(out=causal[:, :], in_=causal[:, :], compare_op=ALU.is_ge, fill=MASKED,
                                   base=0, pattern=[[-1, P]], channel_multiplier=1).then_inc(consts, 1)
                pool.affine_select(out=tri[:, :], in_=ones[:, :], compare_op=ALU.is_gt, fill=0.0,
                                   base=0, pattern=[[1, P]], channel_multiplier=-1).then_inc(consts, 1)
                pool.wait_ge(consts, 8)

        ffn(nc, "f1", X, xn_dram, ys_dram, gate_t, up_t, down_t, router_t, ident, tri, ones, stats, mean, rstd, tmpa, tmpb, NB, E, FC)
        attention(nc, X, w_qkv, w_out, cos_t, sin_t, ident, identb, causal,
                  stats, mean, rstd, tmpa, tmpb, NB)
        ffn(nc, "f2", X, xn_dram, ys_dram, gate_t, up_t, down_t, router_t, ident, tri, ones, stats, mean, rstd, tmpa, tmpb, NB, E, FC)

        stored = sem("stored")
        with nc.Block() as block:
            @block.sync
            def _(sp):
                sp.dma_start(out.rearrange("(n p) d -> p n d", p=P), X[:, :, :]).then_inc(stored, 16)
                sp.wait_ge(stored, 16)


def layernorm_stats(nc, name, ctx, X, stats, mean, rstd, tmpa, tmpb, NB):
    chain_sem = ctx.enter_context(nc.semaphore(name + "_stat_chain"))
    var_ready = ctx.enter_context(nc.semaphore(name + "_var_ready"))
    std_ready = ctx.enter_context(nc.semaphore(name + "_std_ready"))
    with nc.Block() as block:
        @block.vector
        def _(dve):
            link = Chain(dve, chain_sem)
            with dve.Fori(0, NB) as n:
                dve.bn_stats(stats[:, bass.ds(n, 1), :].rearrange("p a s -> p (a s)"),
                             X[:, bass.ds(n, 1), :].rearrange("p a d -> p (a d)")).then_inc(var_ready, 1)
            dve.wait_ge(var_ready, NB)
            me, mo = stats[:, :, 1], stats[:, :, 4]
            link(dve.tensor_tensor(tmpa[:, :], me, mo, ALU.subtract))
            link(dve.tensor_tensor(mean[:, :], me, mo, ALU.add))
            link(dve.tensor_tensor(tmpb[:, :], stats[:, :, 2], stats[:, :, 5], ALU.add))
            link(dve.tensor_tensor(tmpa[:, :], tmpa[:, :], tmpa[:, :], ALU.mult))
            link(dve.tensor_scalar(mean[:, :], mean[:, :], 0.5, None, ALU.mult))
            link(dve.tensor_scalar(tmpb[:, :], tmpb[:, :], 1.0 / P, EPS, ALU.mult, ALU.add))
            dve.scalar_tensor_tensor(out=tmpa[:, :], in0=tmpa[:, :], scalar=0.25, in1=tmpb[:, :],
                                     op0=ALU.mult, op1=ALU.add).then_inc(var_ready, 1)
            dve.wait_ge(std_ready, 1)
            link(dve.reciprocal(rstd[:, :], tmpb[:, :]))
            link(dve.tensor_tensor(tmpb[:, :], rstd[:, :], rstd[:, :], ALU.mult))
            link(dve.tensor_tensor(tmpb[:, :], tmpb[:, :], tmpa[:, :], ALU.mult))
            link(dve.tensor_scalar(tmpb[:, :], tmpb[:, :], -0.5, 1.5, ALU.mult, ALU.add))
            link(dve.tensor_tensor(rstd[:, :], rstd[:, :], tmpb[:, :], ALU.mult))

        @block.scalar
        def _(act):
            act.wait_ge(var_ready, NB + 1)
            act.activation(tmpb[:, :], tmpa[:, :], ACT.Sqrt).then_inc(std_ready, 1)


def row_of(tile, blocks, E):
    return tile[:, :].rearrange("p (a e) -> p a e", a=1).to_broadcast([P, blocks, E])


def ffn(nc, name, X, xn_dram, ys_dram, gate_t, up_t, down_t, router_t, ident, tri, ones,
        stats, mean, rstd, tmpa, tmpb, NB, E, FC):
    GROUPS = NB // 4
    F = FC * P
    BLOCKS = 2 * NB + E - 1
    BLOCKS += BLOCKS % 2
    with ExitStack() as ctx:
        def sb(n, shape, dt=F32, ctx=ctx):
            return ctx.enter_context(nc.sbuf_tensor(f"{name}_{n}", shape, dt))

        def ps(n):
            return ctx.enter_context(nc.psum_tensor(f"{name}_{n}", [P, 512], F32))

        def sem(n):
            return ctx.enter_context(nc.semaphore(f"{name}_{n}"))

        layernorm_stats(nc, name, ctx, X, stats, mean, rstd, tmpa, tmpb, NB)

        gate = sb("gate", [P, 2, E, F], F32R)
        up = sb("up", [P, 2, E, F], F32R)
        down = sb("down", [P, E, FC, P])
        wts = sb("wts", [P, 4, NB])
        source = sb("source", [P, BLOCKS], I32)
        target = sb("target", [P, BLOCKS], I32)
        owner = sb("owner", [P, BLOCKS], I32)
        owners = sb("owners", [P, BLOCKS], I32)
        bank = [ps(f"b{k}") for k in range(8)]

        w_in = sem("w_in")
        w_hi = sem("w_hi")
        w_lo = sem("w_lo")
        w_part = [sem(f"w_part{s}") for s in range(4)]
        with ExitStack() as early:
            router = sb("router", [P, E], ctx=early)
            w_all = sb("w_all", [P, 4, F], ctx=early)
            xn = sb("xn", [P, NB, P], ctx=early)
            xts = [sb(f"xts{k}", [P, 512], ctx=early) for k in range(2)]
            logits = sb("logits", [P, NB, E], ctx=early)
            top8 = sb("top8", [P, NB, 8], ctx=early)
            idx8 = sb("idx8", [P, NB, 8], U32, ctx=early)
            idxf = sb("idxf", [P, NB, 8], ctx=early)
            experts = sb("experts", [P, E], ctx=early)
            experts_i = sb("experts_i", [P, E], I32, ctx=early)
            numbers = sb("numbers", [P, P], ctx=early)
            numbers_i = sb("numbers_i", [P, P], I32, ctx=early)
            numbersb = sb("numbersb", [P, P], BF16, ctx=early)
            place_i = sb("place_i", [P, 2, NB], I32, ctx=early)
            place = sb("place", [P, 2, NB], ctx=early)
            blockf = sb("blockf", [P, 2, NB], ctx=early)
            blockb = sb("blockb", [P, 2, NB], BF16, ctx=early)
            spotb = sb("spotb", [P, 2, NB], BF16, ctx=early)
            tokenp = sb("tokenp", [P, 1], ctx=early)
            tokenp_i = sb("tokenp_i", [P, 1], I32, ctx=early)
            at_spot = sb("at_spot", [P, 2, NB, P], BF16, ctx=early)
            in_block = sb("in_block", [P, 2, NB, BLOCKS], BF16, ctx=early)
            named = sb("named", [P, 2, NB, 2, BLOCKS], BF16, ctx=early)
            found = sb("found", [P, 2, BLOCKS], ctx=early)
            blank = sb("blank", [P, BLOCKS], ctx=early)
            places_f = sb("places_f", [P, BLOCKS], ctx=early)
            chosen = sb("chosen", [P, 2, NB, E], ctx=early)
            both = sb("both", [P, NB, E], ctx=early)
            counts = sb("counts", [P, NB, E], ctx=early)
            row = sb("row", [P, NB, E], ctx=early)
            zeros = sb("zeros", [P, NB], ctx=early)
            total = sb("total", [P, E], ctx=early)
            blocks_i = sb("blocks_i", [P, E], I32, ctx=early)
            blocks_f = sb("blocks_f", [P, E], ctx=early)
            ends = sb("ends", [P, E], ctx=early)
            starts = sb("starts", [P, E], ctx=early)
            past = sb("past", [P, BLOCKS, E], ctx=early)
            ownerf = sb("ownerf", [P, BLOCKS], ctx=early)
            packed = sb("packed", [P, BLOCKS - 4], ctx=early)

            consts = sem("consts")
            xn_ready = sem("xn_ready")
            xn_out = sem("xn_out")
            xt_psum = sem("xt_psum")
            xts_ready = sem("xts_ready")
            lg_psum = sem("lg_psum")
            lg_ready = sem("lg_ready")
            with nc.Block() as block:
                @block.sync
                def _(sp):
                    sp.dma_start(router[:, :], router_t).then_inc(w_in, 16)
                    sp.dma_start(down[:, :, :, :], down_t).then_inc(w_in, 16)
                    for g in range(GROUPS):
                        sp.wait_ge(xn_ready, g + 1)
                        sp.dma_start(xn_dram[4 * g * P:4 * (g + 1) * P, :].rearrange("(n p) d -> p n d", p=P),
                                     xn[:, 4 * g:4 * g + 4, :]).then_inc(xn_out, 16)
                    sp.wait_ge(w_in, 32)
                    sp.wait_ge(xn_out, 16 * GROUPS)

                @block.gpsimd
                def _(pool):
                    pool.iota(experts_i[:, :], pattern=[[1, E]], base=0, channel_multiplier=0).then_inc(consts, 1)
                    pool.iota(numbers_i[:, :], pattern=[[1, P]], base=0,
                              channel_multiplier=0).then_inc(consts, 1)
                    pool.iota(tokenp_i[:, :], pattern=[[0, 1]], base=1,
                              channel_multiplier=1).then_inc(consts, 1)
                    pool.memset(zeros[:, :], 0.0).then_inc(consts, 1)
                    pool.wait_ge(consts, 4)
                    pool.tensor_copy(experts[:, :], experts_i[:, :]).then_inc(consts, 1)
                    pool.tensor_copy(numbers[:, :], numbers_i[:, :]).then_inc(consts, 1)
                    pool.tensor_copy(numbersb[:, :], numbers_i[:, :]).then_inc(consts, 1)
                    pool.tensor_copy(tokenp[:, :], tokenp_i[:, :]).then_inc(consts, 1)
                    pool.wait_ge(consts, 8)

                @block.vector
                def _(dve):
                    def normed(g):
                        for t in range(4):
                            n = g * 4 + t
                            one = dve.tensor_scalar(xn[:, bass.ds(n, 1), :].rearrange("p a d -> p (a d)"),
                                                    X[:, bass.ds(n, 1), :].rearrange("p a d -> p (a d)"),
                                                    mean[:, bass.ds(n, 1)], rstd[:, bass.ds(n, 1)],
                                                    ALU.subtract, ALU.mult)
                        one.then_inc(xn_ready, 1)

                    for g in range(GROUPS):
                        normed(g)
                    for g in range(GROUPS):
                        dve.wait_ge(lg_psum, g + 1)
                        dve.tensor_copy(logits[:, 4 * g:4 * g + 4, :],
                                        bank[2 + g % 2][:, 0:4 * E].rearrange("p (t e) -> p t e", t=4)
                                        ).then_inc(lg_ready, 1)

                @block.scalar
                def _(act):
                    for g in range(GROUPS):
                        act.wait_ge(xt_psum, g + 1)
                        wait(act, lg_psum, g - 1)
                        act.activation(xts[g % 2][:, :], bank[g % 2][:, :], ACT.Copy).then_inc(xts_ready, 1)

                @block.tensor
                def _(pe):
                    def turn(g):
                        pe.wait_ge(xn_ready, g + 1)
                        wait(pe, xts_ready, g - 1)
                        for t in range(4):
                            one = pe.transpose(bank[g % 2][:, t * P:(t + 1) * P], xn[:, 4 * g + t, :], ident[:, :])
                        one.then_inc(xt_psum, 1)

                    pe.wait_ge(w_in, 32)
                    turn(0)
                    for g in range(GROUPS):
                        if g + 1 < GROUPS:
                            turn(g + 1)
                        pe.wait_ge(xts_ready, g + 1)
                        wait(pe, lg_ready, g - 1)
                        for t in range(4):
                            one = pe.matmul(bank[2 + g % 2][:, t * E:(t + 1) * E], xts[g % 2][:, t * P:(t + 1) * P],
                                            router[:, :], start=True, stop=True)
                        one.then_inc(lg_psum, 1)

            chain = sem("chain")
            picked = sem("picked")
            gap_ready = sem("gap_ready")
            exp_ready = sem("exp_ready")
            both_ready = sem("both_ready")
            count_psum = sem("count_psum")
            named_ready = sem("named_ready")
            found_psum = sem("found_psum")
            with nc.Block() as block:
                @block.sync
                def _(sp):
                    for m, t in ((0, gate_t), (1, up_t)):
                        for e in range(E):
                            n = m * E + e
                            wait(sp, w_lo, n - 3)
                            sp.dma_start(w_all[:, n % 4, :], t[:, e, :]).then_inc(w_part[n % 4], 16)

                @block.scalar
                def _(act):
                    for n in range(2 * E):
                        w, e = (gate, up)[n // E], n % E
                        act.wait_ge(w_part[n % 4], 16 * (n // 4) + 16)
                        act.activation(w[:, 0, e, :], w_all[:, n % 4, :], ACT.Copy).then_inc(w_hi, 1)
                    act.wait_ge(gap_ready, 1)
                    act.activation(wts[:, 1, :], wts[:, 0, :], ACT.Exp).then_inc(exp_ready, 1)

                @block.gpsimd
                def _(pool):
                    for n in range(2 * E):
                        w, e = (gate, up)[n // E], n % E
                        pool.wait_ge(w_hi, n + 1)
                        pool.tensor_tensor(w[:, 1, e, :], w_all[:, n % 4, :], w[:, 0, e, :].bitcast(F32),
                                           ALU.subtract).then_inc(w_lo, 1)

                @block.vector
                def _(dve):
                    link = Chain(dve, chain)
                    for n in range(NB):
                        dve.max(top8[:, n, :], logits[:, n, :]).then_inc(picked, 1)
                    dve.wait_ge(picked, NB)
                    for n in range(NB):
                        dve.max_index(idx8[:, n, :], top8[:, n, :], logits[:, n, :]).then_inc(picked, 1)
                    dve.tensor_tensor(wts[:, 0, :], top8[:, :, 1], top8[:, :, 0], ALU.subtract).then_inc(gap_ready, 1)
                    dve.wait_ge(picked, 2 * NB)
                    link(dve.tensor_copy(idxf[:, :, :], idx8[:, :, :]))
                    for k in range(2):
                        link(dve.tensor_tensor(chosen[:, k, :, :], idxf[:, :, k:k + 1].to_broadcast([P, NB, E]),
                                               row_of(experts, NB, E), ALU.is_equal))
                    dve.tensor_tensor(both[:, :, :], chosen[:, 0, :, :], chosen[:, 1, :, :],
                                      ALU.add).then_inc(both_ready, 1)
                    dve.wait_ge(count_psum, 1)
                    link(dve.tensor_copy(counts[:, :, :], bank[1][:, 0:NB * E].rearrange("p (n e) -> p n e", e=E)))
                    for e in range(E):
                        link(dve.tensor_tensor_scan(row[:, :, e], counts[:, :, e], zeros[:, :], 0.0,
                                                    ALU.add, ALU.add))
                    link(dve.tensor_scalar(total[:, :], row[:, NB - 1, :], float(P - 1), None, ALU.add))
                    link(dve.tensor_copy(blocks_i[:, :], total[:, :]))
                    link(dve.tensor_scalar(blocks_i[:, :], blocks_i[:, :], 7, None, ALU.arith_shift_right))
                    link(dve.tensor_copy(blocks_f[:, :], blocks_i[:, :]))
                    link(dve.tensor_tensor_scan(ends[:, :], blocks_f[:, :], zeros[:, 0:E], 0.0, ALU.add, ALU.add))
                    link(dve.tensor_tensor(starts[:, :], ends[:, :], blocks_f[:, :], ALU.subtract))
                    link(dve.tensor_scalar(starts[:, :], starts[:, :], float(P), None, ALU.mult))
                    link(dve.tensor_tensor(row[:, :, :], row[:, :, :], counts[:, :, :], ALU.subtract))
                    link(dve.tensor_tensor(row[:, :, :], bank[0][:, 0:NB * E].rearrange("p (n e) -> p n e", e=E),
                                           row[:, :, :], ALU.add))
                    link(dve.tensor_tensor(row[:, :, :], row[:, :, :], row_of(starts, NB, E), ALU.add))
                    for k in range(2):
                        link(dve.tensor_tensor(chosen[:, k, :, :], chosen[:, k, :, :], row[:, :, :], ALU.mult))
                        link(dve.tensor_reduce(idxf[:, :, k], chosen[:, k, :, :], axis=AX, op=ALU.add))
                        link(dve.tensor_copy(place_i[:, k, :], idxf[:, :, k]))
                        link(dve.tensor_copy(place[:, k, :], idxf[:, :, k]))
                    link(dve.tensor_scalar(place_i[:, :, :], place_i[:, :, :], 7, None, ALU.arith_shift_right))
                    link(dve.tensor_copy(blockf[:, :, :], place_i[:, :, :]))
                    link(dve.tensor_copy(blockb[:, :, :], blockf[:, :, :]))
                    link(dve.scalar_tensor_tensor(out=spotb[:, :, :], in0=blockf[:, :, :], scalar=-float(P),
                                                  in1=place[:, :, :], op0=ALU.mult, op1=ALU.add))
                    for k in range(2):
                        link(dve.tensor_tensor(at_spot[:, k, :, :], row_of(numbersb, NB, P),
                                               spotb[:, k, :].rearrange("p (n a) -> p n a", a=1)
                                               .to_broadcast([P, NB, P]), ALU.is_equal))
                        link(dve.tensor_tensor(in_block[:, k, :, :], row_of(numbersb[:, 0:BLOCKS], NB, BLOCKS),
                                               blockb[:, k, :].rearrange("p (n a) -> p n a", a=1)
                                               .to_broadcast([P, NB, BLOCKS]), ALU.is_equal))
                        link(dve.tensor_tensor(named[:, k, :, 0, :], in_block[:, k, :, :],
                                               numbersb[:, k * NB:(k + 1) * NB]
                                               .rearrange("p (n a) -> p n a", a=1)
                                               .to_broadcast([P, NB, BLOCKS]), ALU.mult))
                        dve.tensor_scalar(named[:, k, :, 1, :], in_block[:, k, :, :], tokenp[:, 0:1], None,
                                          ALU.mult).then_inc(named_ready, 1)
                    link(dve.tensor_tensor(past[:, :, :],
                                           numbers[:, 0:BLOCKS].rearrange("p (b a) -> p b a", a=1)
                                           .to_broadcast([P, BLOCKS, E]),
                                           row_of(ends, BLOCKS, E), ALU.is_ge))
                    link(dve.tensor_reduce(ownerf[:, :], past[:, :, :], axis=AX, op=ALU.add))
                    link(dve.tensor_scalar(ownerf[:, :], ownerf[:, :], float(E - 1), None, ALU.min))
                    link(dve.tensor_copy(owner[:, :], ownerf[:, :]))
                    link(dve.tensor_copy(packed[:, :], ownerf[:, 0:BLOCKS - 4]))
                    for digit, ahead in ((1, 1), (2, 3), (3, 4)):
                        link(dve.scalar_tensor_tensor(out=packed[:, :], in0=ownerf[:, ahead:BLOCKS - 4 + ahead],
                                                      scalar=float(E ** digit), in1=packed[:, :],
                                                      op0=ALU.mult, op1=ALU.add))
                    link(dve.tensor_copy(owners[:, 0:BLOCKS - 4], packed[:, :]))
                    dve.wait_ge(found_psum, 1)
                    link(dve.tensor_copy(found[:, :, :], bank[2][:, 0:2 * BLOCKS].rearrange("p (a b) -> p a b", a=2)))
                    link(dve.tensor_scalar(blank[:, :], found[:, 1, :], 0.0, None, ALU.is_equal))
                    link(dve.tensor_scalar(places_f[:, :], numbers[:, 0:BLOCKS], float(P), float(2 * NB * P),
                                           ALU.mult, ALU.add))
                    link(dve.tensor_scalar(places_f[:, :], places_f[:, :], tokenp[:, 0:1], None, ALU.add))
                    link(dve.tensor_tensor(places_f[:, :], places_f[:, :], blank[:, :], ALU.mult))
                    link(dve.tensor_tensor(places_f[:, :], places_f[:, :], found[:, 1, :], ALU.add))
                    link(dve.scalar_tensor_tensor(out=places_f[:, :], in0=found[:, 0, :], scalar=float(P),
                                                  in1=places_f[:, :], op0=ALU.mult, op1=ALU.add))
                    link(dve.tensor_scalar(target[:, :], places_f[:, :], -1.0, None, ALU.add))
                    link(dve.tensor_scalar(blank[:, :], found[:, 0, :], float(NB), None, ALU.is_ge))
                    link(dve.scalar_tensor_tensor(out=found[:, 0, :], in0=blank[:, :], scalar=-float(NB),
                                                  in1=found[:, 0, :], op0=ALU.mult, op1=ALU.add))
                    link(dve.scalar_tensor_tensor(out=found[:, 0, :], in0=found[:, 0, :], scalar=float(P),
                                                  in1=found[:, 1, :], op0=ALU.mult, op1=ALU.add))
                    link(dve.tensor_scalar(source[:, :], found[:, 0, :], -1.0, 0.0, ALU.add, ALU.max))
                    dve.wait_ge(exp_ready, 1)
                    link(dve.tensor_scalar(wts[:, 2, :], wts[:, 1, :], 1.0, None, ALU.add))
                    link(dve.reciprocal(wts[:, 2, :], wts[:, 2, :]))
                    link(dve.tensor_scalar(wts[:, 2, :], wts[:, 2, :], 0.5, None, ALU.mult))
                    link(dve.tensor_tensor(wts[:, 3, :], wts[:, 2, :], wts[:, 1, :], ALU.mult))

                @block.tensor
                def _(pe):
                    pe.wait_ge(both_ready, 1)
                    every = both[:, :, :].rearrange("p n e -> p (n e)")
                    pe.matmul(bank[0][:, 0:NB * E], tri[:, :], every, start=True, stop=True)
                    pe.matmul(bank[1][:, 0:NB * E], ones[:, :], every, start=True, stop=True).then_inc(count_psum, 1)
                    for k in range(2):
                        pe.wait_ge(named_ready, k + 1)
                        for n in range(NB):
                            m = k * NB + n
                            one = pe.matmul(bank[2][:, 0:2 * BLOCKS], at_spot[:, k, n, :],
                                            named[:, k, n, :, :].rearrange("p a b -> p (a b)"),
                                            start=(m == 0), stop=(m == 2 * NB - 1))
                    one.then_inc(found_psum, 1)

        xb = [sb(f"xb{k}", [P, P]) for k in range(2)]
        xt = [sb(f"xt{k}", [P, 2, P], F32R) for k in range(2)]
        silu = [sb(f"silu{k}", [P, F]) for k in range(2)]
        hid = [sb(f"hid{k}", [P, F]) for k in range(2)]
        hidT = [sb(f"hidT{k}", [P, FC, P]) for k in range(2)]
        y = [sb(f"y{k}", [P, P]) for k in range(2)]
        gate_bank, up_bank, hid_bank, x_bank, y_bank = bank[0:2], bank[2:4], bank[4:6], bank[6], bank[7]

        xb_in = [sem(f"xb_in{k}") for k in range(2)]
        xt_psum = sem("xt_psum2")
        xhi_ready = sem("xhi_ready")
        xlo_ready = sem("xlo_ready")
        gu_psum = sem("gu_psum")
        silu_ready = sem("silu_ready")
        hid_ready = sem("hid_ready")
        hidT_psum = sem("hidT_psum")
        hidT_ready = sem("hidT_ready")
        y_psum = sem("y_psum")
        y_ready = sem("y_ready")
        y_out = [sem(f"y_out{k}") for k in range(2)]

        def program(eng, step, before_two=None):
            for j in range(-1, 4):
                step(eng, j, j % 2)
            with eng.Fori(0, (BLOCKS - 6) // 2) as m:
                known = [before_two(m * 2 + 4)] if before_two else []
                step(eng, m * 2 + 4, 0, *known)
                step(eng, m * 2 + 5, 1, *known)
            for j in range(BLOCKS - 2, BLOCKS + 3):
                step(eng, j, j % 2)

        def has(j, d):
            return not isinstance(j, int) or 0 <= j + d < BLOCKS

        def uses(j, k):
            return (j - k) // 2

        with nc.Block() as block:
            @block.gpsimd
            def _(pool):
                def gather(j):
                    k = j % 2
                    wait(pool, xt_psum, j - 1)
                    pool.indirect_dma_start(
                        out=xb[k][:, :], out_offset=None, in_=xn_dram,
                        in_offset=bass.IndirectOffsetOnAxis(ap=source[:, j:j + 1], axis=0)).then_inc(xb_in[k], 16)

                def scatter(j):
                    k = j % 2
                    pool.wait_ge(y_ready, j + 1)
                    pool.indirect_dma_start(
                        out=ys_dram, out_offset=bass.IndirectOffsetOnAxis(ap=target[:, j:j + 1], axis=0),
                        in_=y[k][:, :], in_offset=None).then_inc(y_out[k], 16)

                gather(0)
                gather(1)
                for j in range(BLOCKS + 3):
                    if j + 2 < BLOCKS:
                        gather(j + 2)
                    if j >= 3:
                        scatter(j - 3)
                for k in range(2):
                    pool.wait_ge(y_out[k], 16 * (BLOCKS // 2))

            @block.tensor
            def _(pe):
                def turn_rows(j, k):
                    pe.wait_ge(xb_in[k], 16 * uses(j, k) + 16)
                    wait(pe, xlo_ready, j)
                    pe.transpose(x_bank[:, 0:P], xb[k][:, :], ident[:, :]).then_inc(xt_psum, 1)

                def project(j, k, e):
                    pe.wait_ge(xlo_ready, j + 1)
                    wait(pe, hid_ready, j - 1)
                    hi, lo = xt[k][:, 0, :], xt[k][:, 1, :]
                    for w, o in ((gate, gate_bank[k]), (up, up_bank[k])):
                        wh = w[:, 0, bass.ds(e, 1), :].rearrange("p a f -> p (a f)")
                        wl = w[:, 1, bass.ds(e, 1), :].rearrange("p a f -> p (a f)")
                        pe.matmul(o[:, :], hi, wh, start=True, stop=False)
                        pe.matmul(o[:, :], hi, wl, start=False, stop=False)
                        one = pe.matmul(o[:, :], lo, wh, start=False, stop=True)
                        one.then_inc(gu_psum, 1)

                def turn_hidden(j, k):
                    pe.wait_ge(hid_ready, j + 1)
                    wait(pe, hidT_ready, j - 1)
                    for c in range(FC):
                        one = pe.transpose(hid_bank[k][:, c * P:(c + 1) * P], hid[k][:, c * P:(c + 1) * P],
                                           ident[:, :])
                    one.then_inc(hidT_psum, 1)

                def project_down(j, k, e):
                    pe.wait_ge(hidT_ready, j + 1)
                    wait(pe, y_ready, j)
                    for c in range(FC):
                        one = pe.matmul(y_bank[:, 0:P], hidT[k][:, c, :],
                                        down[:, bass.ds(e, 1), c, :].rearrange("p a d -> p (a d)"),
                                        start=(c == 0), stop=(c == FC - 1))
                    one.then_inc(y_psum, 1)

                def expert_of(j):
                    return pe.value_load(owner[0:1, bass.ds(j, 1)], min_val=0, max_val=E - 1)

                def two_owners(j):
                    four = pe.value_load(owners[0:1, bass.ds(j - 3, 1)], min_val=0, max_val=E ** 4 - 1)
                    return [four // E ** d % E for d in range(4)]

                def step(pe, j, k, four=None):
                    if four is None:
                        here = expert_of(j) if has(j, 0) else None
                        ending = expert_of(j - 3) if has(j, -3) else None
                    else:
                        ending, here = four[k], four[2 + k]
                    if has(j, -2):
                        turn_hidden(j - 2, k)
                    if has(j, 1):
                        turn_rows(j + 1, 1 - k)
                    if has(j, -3):
                        project_down(j - 3, 1 - k, ending)
                    if has(j, 0):
                        project(j, k, here)
                program(pe, step, two_owners)

            @block.scalar
            def _(act):
                def step(act, j, k):
                    if has(j, -2):
                        act.wait_ge(hidT_psum, j - 1)
                        wait(act, y_psum, j - 3)
                        act.activation(hidT[k][:, :, :], hid_bank[k][:, :].rearrange("p (c q) -> p c q", q=P),
                                       ACT.Copy).then_inc(hidT_ready, 1)
                    if has(j, 1):
                        act.wait_ge(xt_psum, j + 2)
                        wait(act, gu_psum, 2 * (j - 1) + 2)
                        act.activation(xt[1 - k][:, 0, :], x_bank[:, 0:P], ACT.Copy).then_inc(xhi_ready, 1)
                    if has(j, -3):
                        act.wait_ge(y_psum, j - 2)
                        wait(act, y_out[1 - k], 16 * uses(j - 3, 1 - k))
                        act.activation(y[1 - k][:, :], y_bank[:, 0:P], ACT.Copy).then_inc(y_ready, 1)
                    if has(j, 0):
                        act.wait_ge(gu_psum, 2 * j + 1)
                        wait(act, hid_ready, j - 1)
                        act.activation(silu[k][:, :], gate_bank[k][:, :], ACT.Silu).then_inc(silu_ready, 1)
                program(act, step)

            @block.vector
            def _(dve):
                def step(dve, j, k):
                    if has(j, 1):
                        dve.wait_ge(xhi_ready, j + 2)
                        dve.tensor_tensor(xt[1 - k][:, 1, :], x_bank[:, 0:P], xt[1 - k][:, 0, :].bitcast(F32),
                                          ALU.subtract).then_inc(xlo_ready, 1)
                    if has(j, 0):
                        dve.wait_ge(silu_ready, j + 1)
                        dve.wait_ge(gu_psum, 2 * j + 2)
                        wait(dve, hidT_psum, j - 1)
                        dve.tensor_tensor(hid[k][:, :], up_bank[k][:, :], silu[k][:, :],
                                          ALU.mult).then_inc(hid_ready, 1)
                program(dve, step)

        got = [sb(f"got{q}", [P, 2, 4, P]) for q in range(2)]
        got_in = [sem(f"got_in{q}") for q in range(2)]
        added = sem("added")
        with nc.Block() as block:
            @block.sync
            def _(sp):
                for g in range(GROUPS):
                    wait(sp, added, 8 * (g - 1))
                    for k in range(2):
                        first = (k * NB + 4 * g) * P
                        sp.dma_start(got[g % 2][:, k, :, :],
                                     ys_dram[first:first + 4 * P, :].rearrange("(n p) d -> p n d", p=P)
                                     ).then_inc(got_in[g % 2], 16)

            @block.vector
            def _(dve):
                for g in range(GROUPS):
                    dve.wait_ge(got_in[g % 2], 32 * (g // 2) + 32)
                    for k in range(2):
                        if k:
                            dve.wait_ge(added, 8 * g + 4)
                        for t in range(4):
                            n = 4 * g + t
                            dve.scalar_tensor_tensor(out=X[:, n, :], in0=got[g % 2][:, k, t, :],
                                                     scalar=wts[:, 2 + k, n:n + 1], in1=X[:, n, :],
                                                     op0=ALU.mult, op1=ALU.add).then_inc(added, 1)


def attention(nc, X, w_qkv, w_out, cos_t, sin_t, ident, identb, causal, stats, mean, rstd, tmpa, tmpb, NB):
    SCALE = HEAD_DIM ** -0.5
    GROUPS = NB // 4
    STEPS = GROUPS * PAIRS
    QKV = 3 * P
    with ExitStack() as ctx:
        def sb(n, shape, dt=F32):
            return ctx.enter_context(nc.sbuf_tensor("at_" + n, shape, dt))

        def ps(n):
            return ctx.enter_context(nc.psum_tensor("at_" + n, [P, 512], F32))

        def sem(n):
            return ctx.enter_context(nc.semaphore("at_" + n))

        layernorm_stats(nc, "at", ctx, X, stats, mean, rstd, tmpa, tmpb, NB)

        XT = sb("XT", [P, 2, NB * P], F32R)
        w_hi = sb("w_hi", [P, PAIRS, QKV], F32R)
        w_lo = sb("w_lo", [P, PAIRS, QKV], F32R)
        wo = sb("wo", [P, PAIRS, P])
        cos = sb("cos", [P, 4, HEAD_DIM])
        sin = sb("sin", [P, 4, HEAD_DIM])
        bank = [ps(f"b{k}") for k in range(8)]

        w_in = sem("w_in")
        w_his = sem("w_his")
        w_los = sem("w_los")
        xn_ready = sem("xn_ready")
        xt_psum = sem("xt_psum")
        hi_ready = sem("hi_ready")
        lo_ready = sem("lo_ready")

        with ExitStack() as early:
            w_all = early.enter_context(nc.sbuf_tensor("at_w_all", [P, PAIRS, QKV], F32))
            xn = [early.enter_context(nc.sbuf_tensor(f"at_xn{k}", [P, 4, P], F32)) for k in range(2)]
            with nc.Block() as block:
                @block.sync
                def _(sp):
                    w_v = w_qkv.rearrange("e (t j c) -> e t j c", t=3, j=PAIRS)
                    for t in range(3):
                        sp.dma_start(w_all[:, :, t * P:(t + 1) * P], w_v[:, t, :, :]).then_inc(w_in, 16)
                    sp.dma_start(wo[:, :, :], w_out.rearrange("(j f) e -> f j e", f=P)).then_inc(w_in, 16)
                    sp.dma_start(cos[:, :, :], cos_t).then_inc(w_in, 16)
                    sp.dma_start(sin[:, :, :], sin_t).then_inc(w_in, 16)
                    sp.wait_ge(w_in, 96)

                @block.gpsimd
                def _(pool):
                    for j in range(PAIRS):
                        pool.wait_ge(w_his, j + 1)
                        pool.tensor_tensor(w_lo[:, j, :], w_all[:, j, :], w_hi[:, j, :].bitcast(F32),
                                           ALU.subtract).then_inc(w_los, 1)
                    pool.wait_ge(w_los, PAIRS)

                @block.vector
                def _(dve):
                    with dve.Fori(0, GROUPS // 2) as gg:
                        for k in range(2):
                            g = gg * 2 + k
                            for t in range(4):
                                n = g * 4 + t
                                one = dve.tensor_scalar(xn[k][:, t, :],
                                                        X[:, bass.ds(n, 1), :].rearrange("p a d -> p (a d)"),
                                                        mean[:, bass.ds(n, 1)], rstd[:, bass.ds(n, 1)],
                                                        ALU.subtract, ALU.mult)
                            one.then_inc(xn_ready, 1)
                            dve.wait_ge(hi_ready, g + 1)
                            cols = bass.ds(g * 512, 512)
                            dve.tensor_tensor(XT[:, 1, cols], bank[k][:, :], XT[:, 0, cols].bitcast(F32),
                                              ALU.subtract).then_inc(lo_ready, 1)

                @block.scalar
                def _(act):
                    act.wait_ge(w_in, 96)
                    for j in range(PAIRS):
                        act.activation(w_hi[:, j, :], w_all[:, j, :], ACT.Copy).then_inc(w_his, 1)
                    with act.Fori(0, GROUPS // 2) as gg:
                        for k in range(2):
                            g = gg * 2 + k
                            act.wait_ge(xt_psum, g + 1)
                            act.activation(XT[:, 0, bass.ds(g * 512, 512)], bank[k][:, :],
                                           ACT.Copy).then_inc(hi_ready, 1)

                @block.tensor
                def _(pe):
                    with pe.Fori(0, GROUPS // 2) as gg:
                        for k in range(2):
                            g = gg * 2 + k
                            pe.wait_ge(xn_ready, g + 1)
                            for t in range(4):
                                one = pe.transpose(bank[k][:, t * P:(t + 1) * P], xn[k][:, t, :], ident[:, :])
                            one.then_inc(xt_psum, 1)

        xs = sb("xs", [P, 2, 512], F32R)
        ra = [sb(f"ra{k}", [P, 4, HEAD_DIM]) for k in range(2)]
        rb = [sb(f"rb{k}", [P, 4, HEAD_DIM]) for k in range(2)]
        R = sb("R", [P, 4, 2, P])
        QT = [sb(f"QT{k}", [P, 512]) for k in range(2)]
        KT = [[sb(f"KT{k}{h}", [P, 512]) for h in range(2)] for k in range(2)]
        v_new = sb("v_new", [P, 4, P])
        V = [sb(f"V{k}", [P, 4, P]) for k in range(2)]
        prob = [sb(f"prob{k}", [P, 512]) for k in range(4)]
        probT = [sb(f"probT{k}", [P, 4, P]) for k in range(4)]
        OT = sb("OT", [P, 512])
        mx = sb("mx", [P, 4])
        nb = sb("nb", [P, 4])
        sums = sb("sums", [P, 4])
        rec = sb("rec", [P, 4])
        qkv_bank, s_bank, pt_bank = bank[0:2], bank[2:4], bank[4:6]
        o_bank, misc = bank[6], bank[7]

        kt_zero = sem("kt_zero")
        xs_in = sem("xs_in")
        qkv_psum = sem("qkv_psum")
        rope_ready = sem("rope_ready")
        v_ready = sem("v_ready")
        v_moved = sem("v_moved")
        r_ready = sem("r_ready")
        qt_psum = sem("qt_psum")
        kt_psum = sem("kt_psum")
        qt_ready = sem("qt_ready")
        kt_ready = sem("kt_ready")
        s_psum = sem("s_psum")
        mx_ready = sem("mx_ready")
        nb_ready = sem("nb_ready")
        exp_ready = sem("exp_ready")
        rec_ready = sem("rec_ready")
        prob_ready = sem("prob_ready")
        pt_psum = sem("pt_psum")
        ptA_ready = sem("ptA_ready")
        ptB_ready = sem("ptB_ready")
        pv_psum = sem("pv_psum")
        ot_ready = sem("ot_ready")
        y_psum = sem("y_psum")
        y_used = sem("y_used")
        pt_ready = (ptA_ready, ptB_ready)

        def program(eng, step):
            for i in (-1, 0, 1):
                step(eng, i, i % 2)
            with eng.Fori(0, (STEPS - 4) // 2) as k:
                step(eng, k * 2 + 2, 0)
                step(eng, k * 2 + 3, 1)
            for i in (STEPS - 2, STEPS - 1, STEPS):
                step(eng, i, i % 2)

        def has(i, j):
            return not isinstance(i, int) or 0 <= i + j < STEPS

        with nc.Block() as block:
            @block.sync
            def _(sp):
                def step(sp, i, kk):
                    if has(i, 1):
                        wait(sp, qkv_psum, 4 * i + 4)
                        g = (i + 1) // PAIRS
                        sp.dma_start(xs[:, :, :].bitcast(F32),
                                     XT[:, :, bass.ds(g * 512, 512)].bitcast(F32)).then_inc(xs_in, 16)
                        sp.wait_ge(v_ready, 4 * i + 8)
                        wait(sp, pv_psum, 4 * i)
                        sp.dma_start(V[1 - kk][:, :, :], v_new[:, :, :]).then_inc(v_moved, 16)
                program(sp, step)
                sp.wait_ge(xs_in, 16 * STEPS)
                sp.wait_ge(v_moved, 16 * STEPS)

            @block.gpsimd
            def _(pool):
                for k in range(2):
                    pool.memset(KT[k][0][64:128, :], 0.0).then_inc(kt_zero, 1)
                    pool.memset(KT[k][1][0:64, :], 0.0).then_inc(kt_zero, 1)

                def step(pool, i, kk):
                    if has(i, 1):
                        wait(pool, kt_psum, i + 1)
                        for t in range(4):
                            pool.wait_ge(rope_ready, 4 * (i + 1) + t + 1)
                            o = R[:, t, :, :].rearrange("p a (c two) -> p (a c) two", two=2)
                            a = ra[t % 2][:, :, :].rearrange("p h (c two) -> p (h c) two", two=2)
                            b = rb[t % 2][:, :, :].rearrange("p h (c two) -> p (h c) two", two=2)
                            for z in range(2):
                                one = pool.tensor_tensor(o[:, :, z], a[:, :, z], b[:, :, 1 - z], ALU.add)
                            one.then_inc(r_ready, 1)
                program(pool, step)

            @block.tensor
            def _(pe):
                def project(i, t):
                    if t == 0:
                        pe.wait_ge(xs_in, 16 * i + 16)
                    wait(pe, v_ready, 4 * i + t - 1)
                    j = i % PAIRS
                    hi, lo = xs[:, 0, t * P:(t + 1) * P], xs[:, 1, t * P:(t + 1) * P]
                    wh = w_hi[:, bass.ds(j, 1), :].rearrange("p a c -> p (a c)")
                    wl = w_lo[:, bass.ds(j, 1), :].rearrange("p a c -> p (a c)")
                    o = qkv_bank[t % 2][:, 0:QKV]
                    pe.matmul(o, hi, wh, start=True, stop=False)
                    pe.matmul(o, hi, wl, start=False, stop=False)
                    pe.matmul(o, lo, wh, start=False, stop=True).then_inc(qkv_psum, 1)

                def turn(i, which):
                    if which == 0:
                        pe.wait_ge(r_ready, 4 * i + 4)
                        wait(pe, y_used, i - 2)
                    else:
                        pe.wait_ge(qt_ready, i + 1)
                    for t in range(4):
                        one = pe.transpose(misc[:, t * P:(t + 1) * P], R[:, t, which, :], ident[:, :])
                    one.then_inc((qt_psum, kt_psum)[which], 1)

                def scores(i, kk, u):
                    qb, h = divmod(u, 2)
                    U = 8 * i + u
                    if u == 0:
                        pe.wait_ge(kt_ready, i + 1)
                    wait(pe, exp_ready, U - 1)
                    n = (qb + 1) * P
                    pe.matmul(s_bank[h][:, 0:n], QT[kk][:, qb * P:n], KT[kk][h][:, 0:n], start=True, stop=False)
                    pe.matmul(s_bank[h][:, qb * P:n], identb[:, :], causal[:, :], start=False,
                              stop=True).then_inc(s_psum, 1)

                def turn_probs(i, u):
                    qb, h = divmod(u, 2)
                    U = 8 * i + u
                    pe.wait_ge(prob_ready, U + 1)
                    wait(pe, pt_ready[h], 4 * i + qb)
                    for b in range(qb + 1):
                        one = pe.transpose(pt_bank[h][:, b * P:(b + 1) * P], prob[u % 4][:, b * P:(b + 1) * P],
                                           ident[:, :])
                    one.then_inc(pt_psum, 1)

                def weigh(i, kk, qb):
                    if qb == 0:
                        pe.wait_ge(v_moved, 16 * i + 16)
                        wait(pe, ot_ready, i)
                    pe.wait_ge(ptA_ready, 4 * i + qb + 1)
                    pe.wait_ge(ptB_ready, 4 * i + qb + 1)
                    for b in range(qb + 1):
                        for h in range(2):
                            one = pe.matmul(o_bank[64 * h:64 * h + 64, qb * P:(qb + 1) * P],
                                            V[kk][:, b, 64 * h:64 * h + 64],
                                            probT[(2 * qb + h) % 4][:, b, :], start=(b == 0), stop=(b == qb))
                    one.then_inc(pv_psum, 1)

                def out_project(i, last):
                    pe.wait_ge(ot_ready, i + 1)
                    if last:
                        wait(pe, y_used, i)
                    else:
                        pe.wait_ge(kt_ready, i + 3)
                    j = i % PAIRS
                    for t in range(4):
                        one = pe.matmul(misc[:, t * P:(t + 1) * P], OT[:, t * P:(t + 1) * P],
                                        wo[:, bass.ds(j, 1), :].rearrange("p a c -> p (a c)"),
                                        start=True, stop=True)
                    one.then_inc(y_psum, 1)

                def step(pe, i, kk):
                    for u in range(8):
                        if has(i, 0):
                            scores(i, kk, u)
                        if has(i, 1) and u < 4:
                            project(i + 1, u)
                        if has(i, 1) and u in (5, 6):
                            turn(i + 1, u - 5)
                        if u == 7 and has(i, -1):
                            out_project(i - 1, not has(i, 1))
                        if u < 3 and has(i, -1):
                            turn_probs(i - 1, u + 5)
                        if u >= 3 and has(i, 0):
                            turn_probs(i, u - 3)
                        if u in (0, 2, 4) and has(i, -1):
                            weigh(i - 1, 1 - kk, 1 + u // 2)
                        if u == 6 and has(i, 0):
                            weigh(i, kk, 0)
                pe.wait_ge(kt_zero, 4)
                program(pe, step)

            @block.vector
            def _(dve):
                def rope(i, t):
                    dve.wait_ge(qkv_psum, 4 * i + t + 1)
                    wait(dve, r_ready, 4 * i + t - 1)
                    qk = qkv_bank[t % 2][:, 0:4 * HEAD_DIM].rearrange("p (h c) -> p h c", h=4)
                    for dst, table in ((ra, cos), (rb, sin)):
                        one = dve.tensor_tensor(dst[t % 2][:, :, :], qk,
                                                table[:, t:t + 1, :].to_broadcast([P, 4, HEAD_DIM]), ALU.mult)
                    one.then_inc(rope_ready, 1)

                def maximum(i, u):
                    qb, h = divmod(u, 2)
                    U = 8 * i + u
                    c = u % 4
                    dve.wait_ge(s_psum, U + 1)
                    dve.reduce_max(mx[:, c:c + 1], s_bank[h][:, 0:(qb + 1) * P], AX).then_inc(mx_ready, 1)
                    dve.wait_ge(mx_ready, U + 1)
                    dve.tensor_scalar(nb[:, c:c + 1], mx[:, c:c + 1], -SCALE, None, ALU.mult).then_inc(nb_ready, 1)

                def normalise(i, u):
                    qb, h = divmod(u, 2)
                    U = 8 * i + u
                    c = u % 4
                    dve.wait_ge(exp_ready, U + 1)
                    dve.reciprocal(rec[:, c:c + 1], sums[:, c:c + 1]).then_inc(rec_ready, 1)
                    dve.wait_ge(rec_ready, U + 1)
                    w = prob[c][:, 0:(qb + 1) * P]
                    dve.tensor_scalar(w, w, rec[:, c:c + 1], None, ALU.mult).then_inc(prob_ready, 1)

                def copy_b(i, u):
                    qb, h = divmod(u, 2)
                    dve.wait_ge(pt_psum, 8 * i + u + 1)
                    wait(dve, pv_psum, 4 * i + qb - 1)
                    dve.tensor_copy(probT[u % 4][:, 0:qb + 1, :],
                                    pt_bank[h][:, 0:(qb + 1) * P].rearrange("p (b q) -> p b q", q=P)
                                    ).then_inc(ptB_ready, 1)

                def residual(i):
                    dve.wait_ge(y_psum, i + 1)
                    wait(dve, y_used, i)
                    tok = X[:, bass.ds((i // PAIRS) * 4, 4), :]
                    dve.tensor_tensor(tok, misc[:, :].rearrange("p (t d) -> p t d", t=4), tok,
                                      ALU.add).then_inc(y_used, 1)

                def step(dve, i, kk):
                    for u in range(8):
                        if has(i, 0):
                            maximum(i, u)
                        if has(i, 1) and u < 4:
                            rope(i + 1, u)
                        if u == 0 and has(i, -1):
                            normalise(i - 1, 7)
                        if u > 0 and has(i, 0):
                            normalise(i, u - 1)
                        if u in (1, 3) and has(i, -1):
                            copy_b(i - 1, u + 4)
                        if u in (5, 7) and has(i, 0):
                            copy_b(i, u - 4)
                        if u == 7 and has(i, -1):
                            residual(i - 1)
                program(dve, step)

            @block.scalar
            def _(act):
                def values(i, t):
                    act.wait_ge(rope_ready, 4 * i + t + 1)
                    if t == 0:
                        wait(act, v_moved, 16 * i)
                    act.activation(v_new[:, t, :], qkv_bank[t % 2][:, 2 * P:3 * P], ACT.Copy).then_inc(v_ready, 1)

                def exponent(i, u):
                    qb, h = divmod(u, 2)
                    U = 8 * i + u
                    c = u % 4
                    act.wait_ge(nb_ready, U + 1)
                    wait(act, pt_psum, U - 3)
                    n = (qb + 1) * P
                    act.activation(prob[c][:, 0:n], s_bank[h][:, 0:n], ACT.Exp, bias=nb[:, c:c + 1], scale=SCALE,
                                   accum_out=sums[:, c:c + 1]).then_inc(exp_ready, 1)

                def copy_a(i, u):
                    qb, h = divmod(u, 2)
                    act.wait_ge(pt_psum, 8 * i + u + 1)
                    wait(act, pv_psum, 4 * i + qb - 1)
                    act.activation(probT[u % 4][:, 0:qb + 1, :],
                                   pt_bank[h][:, 0:(qb + 1) * P].rearrange("p (b q) -> p b q", q=P),
                                   ACT.Copy).then_inc(ptA_ready, 1)

                def queries(i, kk):
                    act.wait_ge(qt_psum, i + 1)
                    wait(act, s_psum, 8 * (i - 1))
                    act.activation(QT[kk][:, :], misc[:, :], ACT.Copy).then_inc(qt_ready, 1)

                def keys(i, kk):
                    act.wait_ge(kt_psum, i + 1)
                    wait(act, s_psum, 8 * (i - 1))
                    act.activation(KT[kk][0][0:64, :], misc[0:64, :], ACT.Copy)
                    act.activation(KT[kk][1][64:128, :], misc[64:128, :], ACT.Copy).then_inc(kt_ready, 1)

                def outputs(i):
                    act.wait_ge(pv_psum, 4 * i + 4)
                    wait(act, y_psum, i)
                    act.activation(OT[:, :], o_bank[:, :], ACT.Copy).then_inc(ot_ready, 1)

                def step(act, i, kk):
                    for u in range(8):
                        if has(i, 1) and 1 <= u <= 4:
                            values(i + 1, u - 1)
                        if u in (0, 2) and has(i, -1):
                            copy_a(i - 1, u + 4)
                        if u in (4, 6) and has(i, 0):
                            copy_a(i, u - 4)
                        if u == 5 and has(i, -1):
                            outputs(i - 1)
                        if u == 6 and has(i, 1):
                            queries(i + 1, 1 - kk)
                        if u == 7 and has(i, 1):
                            keys(i + 1, 1 - kk)
                        if has(i, 0):
                            exponent(i, u)
                program(act, step)


def kernel(**inputs):
    import concourse.bacc as bacc
    from concourse.bass_utils import run_bass_kernel_spmd

    x = np.ascontiguousarray(inputs["L0_attn_x"])
    batch, seq, dim = x.shape
    half = np.arange(0, HEAD_DIM, 2)
    freqs = (np.float32(1.0) / np.float32(10000.0) ** (half / HEAD_DIM).astype(np.float32)).astype(np.float32)
    angles = (np.arange(seq).astype(np.float32)[:, None] * freqs[None, :]).astype(np.float32)
    cos = np.repeat(np.cos(angles), 2, axis=1).astype(np.float32)
    sin = np.repeat(np.sin(angles), 2, axis=1).astype(np.float32) * np.tile(np.float32([1, -1]), HEAD_DIM // 2)
    by_position = lambda t: np.ascontiguousarray(t.reshape(seq // P, P, HEAD_DIM).transpose(1, 0, 2))
    down = inputs["L0_ffn_down_w"]
    E, D, F = down.shape
    arrays = {
        "x": x.reshape(batch * seq, dim),
        "w_qkv": np.ascontiguousarray(inputs["L0_attn_W_qkv"]),
        "w_out": np.ascontiguousarray(inputs["L0_attn_W_out"]),
        "router_t": np.ascontiguousarray(inputs["L0_ffn_router_w"].T),
        "gate_t": np.ascontiguousarray(inputs["L0_ffn_gate_w"].transpose(2, 0, 1)),
        "up_t": np.ascontiguousarray(inputs["L0_ffn_up_w"].transpose(2, 0, 1)),
        "down_t": np.ascontiguousarray(down.reshape(E, D, F // P, P).transpose(3, 0, 2, 1)),
        "cos_t": by_position(cos),
        "sin_t": by_position(sin),
    }
    nc = bacc.Bacc("TRN2", target_bir_lowering=False, num_devices=1)
    args = [nc.dram_tensor(k, a.shape, mybir.dt.from_np(a.dtype), kind="ExternalInput").ap()
            for k, a in arrays.items()]
    out = nc.dram_tensor("out", (batch * seq, dim), F32, kind="ExternalOutput").ap()
    macaron(nc, *args, out)
    r = run_bass_kernel_spmd(nc, [arrays], core_ids=[0])
    return r.results[0]["out"].reshape(batch, seq, dim)
```

```python
from contextlib import ExitStack

import numpy as np

import concourse.bass as bass
from concourse import mybir

F32 = mybir.dt.float32
F32R = mybir.dt.float32r
BF16 = mybir.dt.bfloat16
I32 = mybir.dt.int32
U32 = mybir.dt.uint32
ALU = mybir.AluOpType
ACT = mybir.ActivationFunctionType
AX = mybir.AxisListType.X

P = 128
HEADS = 16
HEAD_DIM = 64
PAIRS = HEADS // 2
MASKED = -1.0e30
EPS = 1e-5


def wait(eng, sem, value):
    if isinstance(value, int) and value <= 0:
        return
    eng.wait_ge(sem, value)


class Chain:

    def __init__(self, eng, sem):
        self.eng, self.sem, self.count = eng, sem, 0

    def __call__(self, instruction):
        self.count += 1
        instruction.then_inc(self.sem, 1)
        self.eng.wait_ge(self.sem, self.count)


def macaron(nc, x, w_qkv, w_out, router_t, gate_t, up_t, down_t, cos_t, sin_t, out):
    tokens, D = x.shape
    NB = tokens // P
    E = router_t.shape[1]
    FC = gate_t.shape[2] // P
    assert D == P and cos_t.shape[1] == 4 and E ** 7 < 2 ** 24

    with ExitStack() as top:
        def sb(name, shape, dt=F32, ctx=top):
            return ctx.enter_context(nc.sbuf_tensor(name, shape, dt))

        def sem(name):
            return top.enter_context(nc.semaphore(name))

        X = sb("X", [P, NB, D])
        ident = sb("ident", [P, P])
        identb = sb("identb", [P, P], BF16)
        causal = sb("causal", [P, P], BF16)
        tri = sb("tri", [P, P])
        ones = sb("ones", [P, P])
        xn_dram = nc.dram_tensor("xn_dram", (tokens, D), F32).ap()
        ys_dram = nc.dram_tensor("ys_dram", (2 * tokens + (2 * NB + E) * P, D), F32).ap()
        stats = sb("stats", [P, NB, 6])
        mean = sb("mean", [P, NB])
        rstd = sb("rstd", [P, NB])
        tmpa = sb("tmpa", [P, NB])
        tmpb = sb("tmpb", [P, NB])

        CHUNKS = 4
        loaded = [sem(f"loaded{c}") for c in range(CHUNKS)]
        consts = sem("consts")
        with nc.Block() as block:
            @block.sync
            def _(sp):
                for c in range(CHUNKS):
                    part = slice(c * NB // CHUNKS, (c + 1) * NB // CHUNKS)
                    sp.dma_start(X[:, part, :], x.rearrange("(n p) d -> p n d", p=P)[:, part, :]
                                 ).then_inc(loaded[c], 16)

            @block.gpsimd
            def _(pool):
                pool.memset(ones[:, :], 1.0).then_inc(consts, 1)
                pool.memset(ident[:, :], 0.0).then_inc(consts, 1)
                pool.memset(identb[:, :], 0.0).then_inc(consts, 1)
                pool.memset(causal[:, :], 0.0).then_inc(consts, 1)
                pool.wait_ge(consts, 4)
                for one in (ident, identb):
                    pool.affine_select(out=one[:, :], in_=one[:, :], compare_op=ALU.not_equal, fill=1.0,
                                       base=0, pattern=[[-1, P]], channel_multiplier=1).then_inc(consts, 1)
                pool.affine_select(out=causal[:, :], in_=causal[:, :], compare_op=ALU.is_ge, fill=MASKED,
                                   base=0, pattern=[[-1, P]], channel_multiplier=1).then_inc(consts, 1)
                pool.affine_select(out=tri[:, :], in_=ones[:, :], compare_op=ALU.is_gt, fill=0.0,
                                   base=0, pattern=[[1, P]], channel_multiplier=-1).then_inc(consts, 1)
                pool.wait_ge(consts, 8)

        ffn(nc, "f1", X, xn_dram, ys_dram, gate_t, up_t, down_t, router_t, ident, tri, ones,
            stats, mean, rstd, tmpa, tmpb, NB, E, FC, loaded, None)
        attention(nc, X, w_qkv, w_out, cos_t, sin_t, ident, identb, causal,
                  stats, mean, rstd, tmpa, tmpb, NB)
        ffn(nc, "f2", X, xn_dram, ys_dram, gate_t, up_t, down_t, router_t, ident, tri, ones,
            stats, mean, rstd, tmpa, tmpb, NB, E, FC, None, out)


class Moments:

    def __init__(self, nc, name, ctx, X, stats, mean, rstd, tmpa, tmpb, NB):
        self.chain = ctx.enter_context(nc.semaphore(name + "_stat_chain"))
        self.var_ready = ctx.enter_context(nc.semaphore(name + "_var_ready"))
        self.std_ready = ctx.enter_context(nc.semaphore(name + "_std_ready"))
        self.X, self.stats, self.mean, self.rstd, self.tmpa, self.tmpb, self.NB = \
            X, stats, mean, rstd, tmpa, tmpb, NB

    def by_dve(self, dve, loaded):
        stats, mean, rstd, tmpa, tmpb, NB = self.stats, self.mean, self.rstd, self.tmpa, self.tmpb, self.NB
        link = Chain(dve, self.chain)
        for n in range(NB):
            if loaded and n % (NB // len(loaded)) == 0:
                dve.wait_ge(loaded[n // (NB // len(loaded))], 16)
            dve.bn_stats(stats[:, n, :], self.X[:, n, :]).then_inc(self.var_ready, 1)
        dve.wait_ge(self.var_ready, NB)
        me, mo = stats[:, :, 1], stats[:, :, 4]
        link(dve.tensor_tensor(tmpa[:, :], me, mo, ALU.subtract))
        link(dve.tensor_tensor(mean[:, :], me, mo, ALU.add))
        link(dve.tensor_tensor(tmpb[:, :], stats[:, :, 2], stats[:, :, 5], ALU.add))
        link(dve.tensor_tensor(tmpa[:, :], tmpa[:, :], tmpa[:, :], ALU.mult))
        link(dve.tensor_scalar(mean[:, :], mean[:, :], 0.5, None, ALU.mult))
        link(dve.tensor_scalar(tmpb[:, :], tmpb[:, :], 1.0 / P, EPS, ALU.mult, ALU.add))
        dve.scalar_tensor_tensor(out=tmpa[:, :], in0=tmpa[:, :], scalar=0.25, in1=tmpb[:, :],
                                 op0=ALU.mult, op1=ALU.add).then_inc(self.var_ready, 1)
        dve.wait_ge(self.std_ready, 1)
        link(dve.reciprocal(rstd[:, :], tmpb[:, :]))
        link(dve.tensor_tensor(tmpb[:, :], rstd[:, :], rstd[:, :], ALU.mult))
        link(dve.tensor_tensor(tmpb[:, :], tmpb[:, :], tmpa[:, :], ALU.mult))
        link(dve.tensor_scalar(tmpb[:, :], tmpb[:, :], -0.5, 1.5, ALU.mult, ALU.add))
        link(dve.tensor_tensor(rstd[:, :], rstd[:, :], tmpb[:, :], ALU.mult))

    def by_act(self, act):
        act.wait_ge(self.var_ready, self.NB + 1)
        act.activation(self.tmpb[:, :], self.tmpa[:, :], ACT.Sqrt).then_inc(self.std_ready, 1)


def row_of(tile, blocks, E):
    return tile[:, :].rearrange("p (a e) -> p a e", a=1).to_broadcast([P, blocks, E])


def ffn(nc, name, X, xn_dram, ys_dram, gate_t, up_t, down_t, router_t, ident, tri, ones,
        stats, mean, rstd, tmpa, tmpb, NB, E, FC, loaded, out):
    GROUPS = NB // 4
    F = FC * P
    BLOCKS = 2 * NB + E - 1
    BLOCKS += BLOCKS % 2
    with ExitStack() as ctx:
        def sb(n, shape, dt=F32, ctx=ctx):
            return ctx.enter_context(nc.sbuf_tensor(f"{name}_{n}", shape, dt))

        def ps(n):
            return ctx.enter_context(nc.psum_tensor(f"{name}_{n}", [P, 512], F32))

        def sem(n):
            return ctx.enter_context(nc.semaphore(f"{name}_{n}"))

        moments = Moments(nc, name, ctx, X, stats, mean, rstd, tmpa, tmpb, NB)

        gate = sb("gate", [P, 2, E, F], F32R)
        up = sb("up", [P, 2, E, F], F32R)
        down = sb("down", [P, E, FC, P])
        wts = sb("wts", [P, 4, NB])
        source = sb("source", [P, BLOCKS], I32)
        target = sb("target", [P, BLOCKS], I32)
        owner = sb("owner", [P, BLOCKS], I32)
        owners = sb("owners", [P, BLOCKS], I32)
        xb = [sb(f"xb{k}", [P, P]) for k in range(2)]
        bank = [ps(f"b{k}") for k in range(8)]

        xb_in = [sem(f"xb_in{k}") for k in range(2)]

        def gather(pool, j):
            pool.indirect_dma_start(
                out=xb[j % 2][:, :], out_offset=None, in_=xn_dram,
                in_offset=bass.IndirectOffsetOnAxis(ap=source[:, j:j + 1], axis=0)).then_inc(xb_in[j % 2], 16)

        w_in = sem("w_in")
        w_hi = sem("w_hi")
        w_lo = sem("w_lo")
        w_part = [sem(f"w_part{s}") for s in range(4)]
        with ExitStack() as early:
            router = sb("router", [P, E], ctx=early)
            w_all = sb("w_all", [P, 4, F], ctx=early)
            xn = sb("xn", [P, NB, P], ctx=early)
            xts = [sb(f"xts{k}", [P, 512], ctx=early) for k in range(2)]
            logits = sb("logits", [P, NB, E], ctx=early)
            top8 = sb("top8", [P, NB, 8], ctx=early)
            idx8 = sb("idx8", [P, NB, 8], U32, ctx=early)
            idxf = sb("idxf", [P, NB, 8], ctx=early)
            experts = sb("experts", [P, E], ctx=early)
            experts_i = sb("experts_i", [P, E], I32, ctx=early)
            numbers = sb("numbers", [P, P], ctx=early)
            numbers_i = sb("numbers_i", [P, P], I32, ctx=early)
            numbersb = sb("numbersb", [P, P], BF16, ctx=early)
            place_i = sb("place_i", [P, 2, NB], I32, ctx=early)
            place = sb("place", [P, 2, NB], ctx=early)
            blockf = sb("blockf", [P, 2, NB], ctx=early)
            blockb = sb("blockb", [P, 2, NB], BF16, ctx=early)
            spotb = sb("spotb", [P, 2, NB], BF16, ctx=early)
            tokenp = sb("tokenp", [P, 1], ctx=early)
            tokenp_i = sb("tokenp_i", [P, 1], I32, ctx=early)
            at_spot = sb("at_spot", [P, 2, NB, P], BF16, ctx=early)
            in_block = sb("in_block", [P, 2, NB, BLOCKS], BF16, ctx=early)
            named = sb("named", [P, 2, NB, 2, BLOCKS], BF16, ctx=early)
            found = sb("found", [P, 2, BLOCKS], ctx=early)
            token = sb("token", [P, BLOCKS], ctx=early)
            blank = sb("blank", [P, BLOCKS], ctx=early)
            places_f = sb("places_f", [P, BLOCKS], ctx=early)
            chosen = sb("chosen", [P, 2, NB, E], ctx=early)
            both = sb("both", [P, NB, E], ctx=early)
            counts = sb("counts", [P, NB, E], ctx=early)
            row = sb("row", [P, NB, E], ctx=early)
            zeros = sb("zeros", [P, NB], ctx=early)
            total = sb("total", [P, E], ctx=early)
            blocks_i = sb("blocks_i", [P, E], I32, ctx=early)
            blocks_f = sb("blocks_f", [P, E], ctx=early)
            ends = sb("ends", [P, E], ctx=early)
            starts = sb("starts", [P, E], ctx=early)
            past = sb("past", [P, BLOCKS, E], ctx=early)
            ownerf = sb("ownerf", [P, BLOCKS], ctx=early)
            packed = sb("packed", [P, BLOCKS - 6], ctx=early)

            consts = sem("consts")
            xn_ready = sem("xn_ready")
            xn_out = sem("xn_out")
            xt_psum = sem("xt_psum")
            xts_ready = sem("xts_ready")
            lg_psum = sem("lg_psum")
            lg_ready = sem("lg_ready")
            picked = sem("picked")
            chain = sem("chain")
            gap_ready = sem("gap_ready")
            exp_ready = sem("exp_ready")
            both_ready = sem("both_ready")
            count_psum = sem("count_psum")
            block_named = sem("block_named")
            source_ready = sem("source_ready")
            token_named = sem("token_named")
            spot_ready = sem("spot_ready")
            block_ready = sem("block_ready")
            found_psum = sem("found_psum")
            with nc.Block() as block:
                @block.sync
                def _(sp):
                    sp.dma_start(router[:, :], router_t).then_inc(w_in, 16)
                    sp.dma_start(down[:, :, :, :], down_t).then_inc(w_in, 16)
                    for n in range(2 * E):
                        wait(sp, w_lo, n - 3)
                        sp.dma_start(w_all[:, n % 4, :], (gate_t, up_t)[n // E][:, n % E, :]
                                     ).then_inc(w_part[n % 4], 16)
                    for g in range(GROUPS):
                        sp.wait_ge(xn_ready, g + 1)
                        sp.dma_start(xn_dram[4 * g * P:4 * (g + 1) * P, :].rearrange("(n p) d -> p n d", p=P),
                                     xn[:, 4 * g:4 * g + 4, :]).then_inc(xn_out, 16)
                    sp.wait_ge(w_in, 32)

                @block.gpsimd
                def _(pool):
                    pool.iota(experts_i[:, :], pattern=[[1, E]], base=0, channel_multiplier=0).then_inc(consts, 1)
                    pool.iota(numbers_i[:, :], pattern=[[1, P]], base=0,
                              channel_multiplier=0).then_inc(consts, 1)
                    pool.iota(tokenp_i[:, :], pattern=[[0, 1]], base=1,
                              channel_multiplier=1).then_inc(consts, 1)
                    pool.memset(zeros[:, :], 0.0).then_inc(consts, 1)
                    pool.wait_ge(consts, 4)
                    pool.tensor_copy(experts[:, :], experts_i[:, :]).then_inc(consts, 1)
                    pool.tensor_copy(numbers[:, :], numbers_i[:, :]).then_inc(consts, 1)
                    pool.tensor_copy(numbersb[:, :], numbers_i[:, :]).then_inc(consts, 1)
                    pool.tensor_copy(tokenp[:, :], tokenp_i[:, :]).then_inc(consts, 1)
                    pool.wait_ge(consts, 8)
                    for n in range(2 * E):
                        w, e = (gate, up)[n // E], n % E
                        pool.wait_ge(w_hi, n + 1)
                        pool.tensor_tensor(w[:, 1, e, :], w_all[:, n % 4, :], w[:, 0, e, :].bitcast(F32),
                                           ALU.subtract).then_inc(w_lo, 1)

                @block.vector
                def _(dve):
                    def normed(g):
                        for t in range(4):
                            n = g * 4 + t
                            one = dve.tensor_scalar(xn[:, bass.ds(n, 1), :].rearrange("p a d -> p (a d)"),
                                                    X[:, bass.ds(n, 1), :].rearrange("p a d -> p (a d)"),
                                                    mean[:, bass.ds(n, 1)], rstd[:, bass.ds(n, 1)],
                                                    ALU.subtract, ALU.mult)
                        one.then_inc(xn_ready, 1)

                    moments.by_dve(dve, loaded)
                    for g in range(GROUPS):
                        normed(g)
                    for g in range(GROUPS):
                        dve.wait_ge(lg_psum, g + 1)
                        dve.tensor_copy(logits[:, 4 * g:4 * g + 4, :],
                                        bank[2 + g % 2][:, 0:4 * E].rearrange("p (t e) -> p t e", t=4)
                                        ).then_inc(lg_ready, 1)
                        dve.wait_ge(lg_ready, g + 1)
                        for n in range(4 * g, 4 * g + 4):
                            dve.max(top8[:, n, :], logits[:, n, :]).then_inc(picked, 1)
                        dve.wait_ge(picked, 8 * g + 4)
                        for n in range(4 * g, 4 * g + 4):
                            dve.max_index(idx8[:, n, :], top8[:, n, :], logits[:, n, :]).then_inc(picked, 1)

                @block.scalar
                def _(act):
                    def split(n):
                        w, e = (gate, up)[n // E], n % E
                        act.wait_ge(w_part[n % 4], 16 * (n // 4) + 16)
                        act.activation(w[:, 0, e, :], w_all[:, n % 4, :], ACT.Copy).then_inc(w_hi, 1)

                    moments.by_act(act)
                    for g in range(GROUPS):
                        for n in range(2 * E * g // GROUPS, 2 * E * (g + 1) // GROUPS):
                            if n > 0:
                                split(n - 1)
                        act.wait_ge(xt_psum, g + 1)
                        wait(act, lg_psum, g - 1)
                        act.activation(xts[g % 2][:, :], bank[g % 2][:, :], ACT.Copy).then_inc(xts_ready, 1)
                    split(2 * E - 1)

                @block.tensor
                def _(pe):
                    def turn(g):
                        pe.wait_ge(xn_ready, g + 1)
                        wait(pe, xts_ready, g - 1)
                        for t in range(4):
                            one = pe.transpose(bank[g % 2][:, t * P:(t + 1) * P], xn[:, 4 * g + t, :], ident[:, :])
                        one.then_inc(xt_psum, 1)

                    pe.wait_ge(w_in, 32)
                    turn(0)
                    for g in range(GROUPS):
                        if g + 1 < GROUPS:
                            turn(g + 1)
                        pe.wait_ge(xts_ready, g + 1)
                        wait(pe, lg_ready, g - 1)
                        for t in range(4):
                            one = pe.matmul(bank[2 + g % 2][:, t * E:(t + 1) * E], xts[g % 2][:, t * P:(t + 1) * P],
                                            router[:, :], start=True, stop=True)
                        one.then_inc(lg_psum, 1)

                @block.scalar
                def _(act):
                    act.wait_ge(gap_ready, 1)
                    act.activation(wts[:, 1, :], wts[:, 0, :], ACT.Exp).then_inc(exp_ready, 1)
                    for k in range(2):
                        act.wait_ge(block_ready, k + 1)
                        act.activation(named[:, k, :, 1, :], in_block[:, k, :, :], ACT.Copy,
                                       scale=tokenp[:, 0:1]).then_inc(token_named, 1)

                @block.gpsimd
                def _(pool):
                    for k in range(2):
                        pool.wait_ge(block_ready, k + 1)
                        for n in range(0, NB, NB // 2):
                            some = slice(n, n + NB // 2)
                            number = numbersb[:, k * NB + n:k * NB + n + NB // 2]
                            pool.tensor_tensor(named[:, k, some, 0, :], in_block[:, k, some, :],
                                               number.rearrange("p (n a) -> p n a", a=1)
                                               .to_broadcast([P, NB // 2, BLOCKS]),
                                               ALU.mult).then_inc(block_named, 1)
                    pool.wait_ge(source_ready, 1)
                    pool.wait_ge(xn_out, 16 * GROUPS)
                    gather(pool, 0)
                    gather(pool, 1)

                @block.vector
                def _(dve):
                    link = Chain(dve, chain)
                    dve.wait_ge(picked, 2 * NB)
                    dve.tensor_tensor(wts[:, 0, :], top8[:, :, 1], top8[:, :, 0], ALU.subtract).then_inc(gap_ready, 1)
                    link(dve.tensor_copy(idxf[:, :, :], idx8[:, :, :]))
                    for k in range(2):
                        link(dve.tensor_tensor(chosen[:, k, :, :], idxf[:, :, k:k + 1].to_broadcast([P, NB, E]),
                                               row_of(experts, NB, E), ALU.is_equal))
                    dve.tensor_tensor(both[:, :, :], chosen[:, 0, :, :], chosen[:, 1, :, :],
                                      ALU.add).then_inc(both_ready, 1)
                    dve.wait_ge(count_psum, 1)
                    link(dve.tensor_copy(counts[:, :, :], bank[1][:, 0:NB * E].rearrange("p (n e) -> p n e", e=E)))
                    for e in range(E):
                        link(dve.tensor_tensor_scan(row[:, :, e], counts[:, :, e], zeros[:, :], 0.0,
                                                    ALU.add, ALU.add))
                    link(dve.tensor_scalar(total[:, :], row[:, NB - 1, :], float(P - 1), None, ALU.add))
                    link(dve.tensor_copy(blocks_i[:, :], total[:, :]))
                    link(dve.tensor_scalar(blocks_i[:, :], blocks_i[:, :], 7, None, ALU.arith_shift_right))
                    link(dve.tensor_copy(blocks_f[:, :], blocks_i[:, :]))
                    link(dve.tensor_tensor_scan(ends[:, :], blocks_f[:, :], zeros[:, 0:E], 0.0, ALU.add, ALU.add))
                    link(dve.tensor_tensor(starts[:, :], ends[:, :], blocks_f[:, :], ALU.subtract))
                    link(dve.tensor_scalar(starts[:, :], starts[:, :], float(P), None, ALU.mult))
                    link(dve.tensor_tensor(row[:, :, :], row[:, :, :], counts[:, :, :], ALU.subtract))
                    link(dve.tensor_tensor(row[:, :, :], bank[0][:, 0:NB * E].rearrange("p (n e) -> p n e", e=E),
                                           row[:, :, :], ALU.add))
                    link(dve.tensor_tensor(row[:, :, :], row[:, :, :], row_of(starts, NB, E), ALU.add))
                    for k in range(2):
                        link(dve.tensor_tensor(chosen[:, k, :, :], chosen[:, k, :, :], row[:, :, :], ALU.mult))
                        link(dve.tensor_reduce(idxf[:, :, k], chosen[:, k, :, :], axis=AX, op=ALU.add))
                        link(dve.tensor_copy(place_i[:, k, :], idxf[:, :, k]))
                        link(dve.tensor_copy(place[:, k, :], idxf[:, :, k]))
                    link(dve.tensor_scalar(place_i[:, :, :], place_i[:, :, :], 7, None, ALU.arith_shift_right))
                    link(dve.tensor_copy(blockf[:, :, :], place_i[:, :, :]))
                    link(dve.tensor_copy(blockb[:, :, :], blockf[:, :, :]))
                    link(dve.scalar_tensor_tensor(out=spotb[:, :, :], in0=blockf[:, :, :], scalar=-float(P),
                                                  in1=place[:, :, :], op0=ALU.mult, op1=ALU.add))
                    for k in range(2):
                        dve.tensor_tensor(in_block[:, k, :, :], row_of(numbersb[:, 0:BLOCKS], NB, BLOCKS),
                                          blockb[:, k, :].rearrange("p (n a) -> p n a", a=1)
                                          .to_broadcast([P, NB, BLOCKS]), ALU.is_equal).then_inc(block_ready, 1)
                    for k in range(2):
                        for n in range(0, NB, NB // 4):
                            some = slice(n, n + NB // 4)
                            dve.tensor_tensor(at_spot[:, k, some, :], row_of(numbersb, NB // 4, P),
                                              spotb[:, k, some].rearrange("p (n a) -> p n a", a=1)
                                              .to_broadcast([P, NB // 4, P]), ALU.is_equal).then_inc(spot_ready, 1)
                    link(dve.tensor_tensor(past[:, :, :],
                                           numbers[:, 0:BLOCKS].rearrange("p (b a) -> p b a", a=1)
                                           .to_broadcast([P, BLOCKS, E]),
                                           row_of(ends, BLOCKS, E), ALU.is_ge))
                    link(dve.tensor_reduce(ownerf[:, :], past[:, :, :], axis=AX, op=ALU.add))
                    link(dve.tensor_scalar(ownerf[:, :], ownerf[:, :], float(E - 1), None, ALU.min))
                    link(dve.tensor_copy(owner[:, :], ownerf[:, :]))
                    dve.wait_ge(found_psum, 1)
                    link(dve.tensor_copy(found[:, :, :], bank[2][:, 0:2 * BLOCKS].rearrange("p (a b) -> p a b", a=2)))
                    link(dve.tensor_scalar(blank[:, :], found[:, 0, :], float(NB), None, ALU.is_ge))
                    link(dve.scalar_tensor_tensor(out=token[:, :], in0=blank[:, :], scalar=-float(NB),
                                                  in1=found[:, 0, :], op0=ALU.mult, op1=ALU.add))
                    link(dve.scalar_tensor_tensor(out=token[:, :], in0=token[:, :], scalar=float(P),
                                                  in1=found[:, 1, :], op0=ALU.mult, op1=ALU.add))
                    dve.tensor_scalar(source[:, :], token[:, :], -1.0, 0.0, ALU.add, ALU.max
                                      ).then_inc(source_ready, 1)
                    link(dve.tensor_copy(packed[:, :], ownerf[:, 0:BLOCKS - 6]))
                    for digit in range(1, 7):
                        link(dve.scalar_tensor_tensor(out=packed[:, :], in0=ownerf[:, digit:BLOCKS - 6 + digit],
                                                      scalar=float(E ** digit), in1=packed[:, :],
                                                      op0=ALU.mult, op1=ALU.add))
                    link(dve.tensor_copy(owners[:, 0:BLOCKS - 6], packed[:, :]))
                    link(dve.tensor_scalar(blank[:, :], found[:, 1, :], 0.0, None, ALU.is_equal))
                    link(dve.tensor_scalar(places_f[:, :], numbers[:, 0:BLOCKS], float(P), float(2 * NB * P),
                                           ALU.mult, ALU.add))
                    link(dve.tensor_scalar(places_f[:, :], places_f[:, :], tokenp[:, 0:1], None, ALU.add))
                    link(dve.tensor_tensor(places_f[:, :], places_f[:, :], blank[:, :], ALU.mult))
                    link(dve.tensor_tensor(places_f[:, :], places_f[:, :], found[:, 1, :], ALU.add))
                    link(dve.scalar_tensor_tensor(out=places_f[:, :], in0=found[:, 0, :], scalar=float(P),
                                                  in1=places_f[:, :], op0=ALU.mult, op1=ALU.add))
                    link(dve.tensor_scalar(target[:, :], places_f[:, :], -1.0, None, ALU.add))
                    dve.wait_ge(exp_ready, 1)
                    link(dve.tensor_scalar(wts[:, 2, :], wts[:, 1, :], 1.0, None, ALU.add))
                    link(dve.reciprocal(wts[:, 2, :], wts[:, 2, :]))
                    link(dve.tensor_scalar(wts[:, 2, :], wts[:, 2, :], 0.5, None, ALU.mult))
                    link(dve.tensor_tensor(wts[:, 3, :], wts[:, 2, :], wts[:, 1, :], ALU.mult))

                @block.tensor
                def _(pe):
                    pe.wait_ge(both_ready, 1)
                    every = both[:, :, :].rearrange("p n e -> p (n e)")
                    pe.matmul(bank[0][:, 0:NB * E], tri[:, :], every, start=True, stop=True)
                    pe.matmul(bank[1][:, 0:NB * E], ones[:, :], every, start=True, stop=True).then_inc(count_psum, 1)
                    for k in range(2):
                        pe.wait_ge(token_named, k + 1)
                        for n in range(NB):
                            if n % (NB // 4) == 0:
                                pe.wait_ge(spot_ready, 4 * k + n // (NB // 4) + 1)
                            if n % (NB // 2) == 0:
                                pe.wait_ge(block_named, 2 * k + n // (NB // 2) + 1)
                            m = k * NB + n
                            one = pe.matmul(bank[2][:, 0:2 * BLOCKS], at_spot[:, k, n, :],
                                            named[:, k, n, :, :].rearrange("p a b -> p (a b)"),
                                            start=(m == 0), stop=(m == 2 * NB - 1))
                    one.then_inc(found_psum, 1)

        xt = [sb(f"xt{k}", [P, 2, P], F32R) for k in range(2)]
        silu = [sb(f"silu{k}", [P, F]) for k in range(2)]
        hid = [sb(f"hid{k}", [P, F]) for k in range(2)]
        hidT = [sb(f"hidT{k}", [P, FC, P]) for k in range(2)]
        y = [sb(f"y{k}", [P, P]) for k in range(2)]
        gate_bank, up_bank, hid_bank, x_bank, y_bank = bank[0:2], bank[2:4], bank[4:6], bank[6], bank[7]

        xt_psum = sem("xt_psum2")
        xhi_ready = sem("xhi_ready")
        xlo_ready = sem("xlo_ready")
        gu_psum = sem("gu_psum")
        silu_ready = sem("silu_ready")
        hid_ready = sem("hid_ready")
        hidT_psum = sem("hidT_psum")
        hidT_ready = sem("hidT_ready")
        y_psum = sem("y_psum")
        y_ready = sem("y_ready")
        y_out = [sem(f"y_out{k}") for k in range(2)]

        def program(eng, step, before_four=None):
            loops = (BLOCKS - 6) // 4
            for j in range(-1, 4):
                step(eng, j, j % 2)
            with eng.Fori(0, loops) as m:
                known = before_four(m * 4 + 4) if before_four else None
                for s in range(4):
                    step(eng, m * 4 + 4 + s, s % 2, *([known[s], known[3 + s]] if before_four else []))
            for j in range(4 + 4 * loops, BLOCKS + 3):
                step(eng, j, j % 2)

        def has(j, d):
            return not isinstance(j, int) or 0 <= j + d < BLOCKS

        def uses(j, k):
            return (j - k) // 2

        with nc.Block() as block:
            @block.gpsimd
            def _(pool):
                def scatter(j):
                    k = j % 2
                    pool.wait_ge(y_ready, j + 1)
                    pool.indirect_dma_start(
                        out=ys_dram, out_offset=bass.IndirectOffsetOnAxis(ap=target[:, j:j + 1], axis=0),
                        in_=y[k][:, :], in_offset=None).then_inc(y_out[k], 16)

                for j in range(BLOCKS + 3):
                    if j + 2 < BLOCKS:
                        pool.wait_ge(xt_psum, j + 1)
                        gather(pool, j + 2)
                    if j >= 3:
                        scatter(j - 3)
                for k in range(2):
                    pool.wait_ge(y_out[k], 16 * (BLOCKS // 2))

            @block.tensor
            def _(pe):
                def turn_rows(j, k):
                    pe.wait_ge(xb_in[k], 16 * uses(j, k) + 16)
                    wait(pe, xlo_ready, j)
                    pe.transpose(x_bank[:, 0:P], xb[k][:, :], ident[:, :]).then_inc(xt_psum, 1)

                def project(j, k, e):
                    pe.wait_ge(xlo_ready, j + 1)
                    wait(pe, hid_ready, j - 1)
                    hi, lo = xt[k][:, 0, :], xt[k][:, 1, :]
                    for w, o in ((gate, gate_bank[k]), (up, up_bank[k])):
                        wh = w[:, 0, bass.ds(e, 1), :].rearrange("p a f -> p (a f)")
                        wl = w[:, 1, bass.ds(e, 1), :].rearrange("p a f -> p (a f)")
                        pe.matmul(o[:, :], hi, wh, start=True, stop=False)
                        pe.matmul(o[:, :], hi, wl, start=False, stop=False)
                        one = pe.matmul(o[:, :], lo, wh, start=False, stop=True)
                        one.then_inc(gu_psum, 1)

                def turn_hidden(j, k):
                    pe.wait_ge(hid_ready, j + 1)
                    wait(pe, hidT_ready, j - 1)
                    for c in range(FC):
                        one = pe.transpose(hid_bank[k][:, c * P:(c + 1) * P], hid[k][:, c * P:(c + 1) * P],
                                           ident[:, :])
                    one.then_inc(hidT_psum, 1)

                def project_down(j, k, e):
                    pe.wait_ge(hidT_ready, j + 1)
                    wait(pe, y_ready, j)
                    for c in range(FC):
                        one = pe.matmul(y_bank[:, 0:P], hidT[k][:, c, :],
                                        down[:, bass.ds(e, 1), c, :].rearrange("p a d -> p (a d)"),
                                        start=(c == 0), stop=(c == FC - 1))
                    one.then_inc(y_psum, 1)

                def expert_of(j):
                    return pe.value_load(owner[0:1, bass.ds(j, 1)], min_val=0, max_val=E - 1)

                def seven_owners(j):
                    all_seven = pe.value_load(owners[0:1, bass.ds(j - 3, 1)], min_val=0, max_val=E ** 7 - 1)
                    return [all_seven // E ** d % E for d in range(7)]

                def step(pe, j, k, ending=None, here=None):
                    if isinstance(j, int):
                        here = expert_of(j) if has(j, 0) else None
                        ending = expert_of(j - 3) if has(j, -3) else None
                    if has(j, -2):
                        turn_hidden(j - 2, k)
                    if has(j, 1):
                        turn_rows(j + 1, 1 - k)
                    if has(j, -3):
                        project_down(j - 3, 1 - k, ending)
                    if has(j, 0):
                        project(j, k, here)
                program(pe, step, seven_owners)

            @block.scalar
            def _(act):
                def step(act, j, k):
                    if has(j, -2):
                        act.wait_ge(hidT_psum, j - 1)
                        wait(act, y_psum, j - 3)
                        act.activation(hidT[k][:, :, :], hid_bank[k][:, :].rearrange("p (c q) -> p c q", q=P),
                                       ACT.Copy).then_inc(hidT_ready, 1)
                    if has(j, 1):
                        act.wait_ge(xt_psum, j + 2)
                        wait(act, gu_psum, 2 * (j - 1) + 2)
                        act.activation(xt[1 - k][:, 0, :], x_bank[:, 0:P], ACT.Copy).then_inc(xhi_ready, 1)
                    if has(j, -3):
                        act.wait_ge(y_psum, j - 2)
                        wait(act, y_out[1 - k], 16 * uses(j - 3, 1 - k))
                        act.activation(y[1 - k][:, :], y_bank[:, 0:P], ACT.Copy).then_inc(y_ready, 1)
                    if has(j, 0):
                        act.wait_ge(gu_psum, 2 * j + 1)
                        wait(act, hid_ready, j - 1)
                        act.activation(silu[k][:, :], gate_bank[k][:, :], ACT.Silu).then_inc(silu_ready, 1)
                program(act, step)

            @block.vector
            def _(dve):
                def step(dve, j, k):
                    if has(j, 1):
                        dve.wait_ge(xhi_ready, j + 2)
                        dve.tensor_tensor(xt[1 - k][:, 1, :], x_bank[:, 0:P], xt[1 - k][:, 0, :].bitcast(F32),
                                          ALU.subtract).then_inc(xlo_ready, 1)
                    if has(j, 0):
                        dve.wait_ge(silu_ready, j + 1)
                        dve.wait_ge(gu_psum, 2 * j + 2)
                        wait(dve, hidT_psum, j - 1)
                        dve.tensor_tensor(hid[k][:, :], up_bank[k][:, :], silu[k][:, :],
                                          ALU.mult).then_inc(hid_ready, 1)
                program(dve, step)

        by_pool = [g for g in range(GROUPS) if g % 8 in (1, 3, 6)]
        by_dve = [g for g in range(GROUPS) if g not in by_pool]
        got = [sb(f"got{g}", [P, 2, 4, P]) for g in range(GROUPS)]
        got_in = [sem(f"got_in{g}") for g in range(GROUPS)]
        weighted = sem("weighted")
        dve_added = sem("dve_added")
        pool_added = sem("pool_added")
        stored = sem("stored")

        with nc.Block() as block:
            @block.sync
            def _(sp):
                for g in range(GROUPS):
                    for k in range(2):
                        first = (k * NB + 4 * g) * P
                        sp.dma_start(got[g][:, k, :, :],
                                     ys_dram[first:first + 4 * P, :].rearrange("(n p) d -> p n d", p=P)
                                     ).then_inc(got_in[g], 16)

            @block.gpsimd
            def _(pool):
                for m, g in enumerate(by_pool):
                    for k in range(2):
                        pool.wait_ge(weighted, 8 * m + 4 * k + 4)
                        if k:
                            pool.wait_ge(pool_added, 2 * m + 1)
                        some = X[:, 4 * g:4 * g + 4, :]
                        pool.tensor_tensor(some, got[g][:, k, :, :], some, ALU.add).then_inc(pool_added, 1)

            @block.vector
            def _(dve):
                for m, g in enumerate(by_dve):
                    dve.wait_ge(got_in[g], 32)
                    for k in range(2):
                        if k:
                            dve.wait_ge(dve_added, 8 * m + 4)
                        for t in range(4):
                            n = 4 * g + t
                            dve.scalar_tensor_tensor(out=X[:, n, :], in0=got[g][:, k, t, :],
                                                     scalar=wts[:, 2 + k, n:n + 1], in1=X[:, n, :],
                                                     op0=ALU.mult, op1=ALU.add).then_inc(dve_added, 1)

            @block.scalar
            def _(act):
                for g in by_pool:
                    act.wait_ge(got_in[g], 32)
                    for k in range(2):
                        for t in range(4):
                            n = 4 * g + t
                            act.activation(got[g][:, k, t, :], got[g][:, k, t, :], ACT.Copy,
                                           scale=wts[:, 2 + k, n:n + 1]).then_inc(weighted, 1)
                if out is not None:
                    for g in range(GROUPS):
                        if g in by_pool:
                            act.wait_ge(pool_added, 2 * by_pool.index(g) + 2)
                        else:
                            act.wait_ge(dve_added, 8 * by_dve.index(g) + 8)
                        act.dma_start(out[4 * g * P:4 * (g + 1) * P, :].rearrange("(n p) d -> p n d", p=P),
                                      X[:, 4 * g:4 * g + 4, :]).then_inc(stored, 16)
                    act.wait_ge(stored, 16 * GROUPS)


def attention(nc, X, w_qkv, w_out, cos_t, sin_t, ident, identb, causal, stats, mean, rstd, tmpa, tmpb, NB):
    SCALE = HEAD_DIM ** -0.5
    GROUPS = NB // 4
    STEPS = GROUPS * PAIRS
    QKV = 3 * P
    with ExitStack() as ctx:
        def sb(n, shape, dt=F32):
            return ctx.enter_context(nc.sbuf_tensor("at_" + n, shape, dt))

        def ps(n):
            return ctx.enter_context(nc.psum_tensor("at_" + n, [P, 512], F32))

        def sem(n):
            return ctx.enter_context(nc.semaphore("at_" + n))

        moments = Moments(nc, "at", ctx, X, stats, mean, rstd, tmpa, tmpb, NB)

        XT = sb("XT", [P, 2, NB * P], F32R)
        w_hi = sb("w_hi", [P, PAIRS, QKV], F32R)
        w_lo = sb("w_lo", [P, PAIRS, QKV], F32R)
        wo = sb("wo", [P, PAIRS, P])
        cos_sin = sb("cos_sin", [P, 4, 2, HEAD_DIM])
        s_bank = [ctx.enter_context(nc.psum_tensor(f"at_s{k}", [P, 2, 512], F32)) for k in range(2)]
        bank = [ps(f"b{k}") for k in range(4)]

        w_in = sem("w_in")
        w_his = sem("w_his")
        w_los = sem("w_los")
        xn_ready = sem("xn_ready")
        xt_psum = sem("xt_psum")
        hi_ready = sem("hi_ready")
        lo_ready = sem("lo_ready")

        with ExitStack() as early:
            w_all = early.enter_context(nc.sbuf_tensor("at_w_all", [P, PAIRS, QKV], F32))
            xn = [early.enter_context(nc.sbuf_tensor(f"at_xn{k}", [P, 4, P], F32)) for k in range(2)]
            with nc.Block() as block:
                @block.sync
                def _(sp):
                    w_v = w_qkv.rearrange("e (t j c) -> e t j c", t=3, j=PAIRS)
                    for t in range(3):
                        sp.dma_start(w_all[:, :, t * P:(t + 1) * P], w_v[:, t, :, :]).then_inc(w_in, 16)
                    sp.dma_start(wo[:, :, :], w_out.rearrange("(j f) e -> f j e", f=P)).then_inc(w_in, 16)
                    sp.dma_start(cos_sin[:, :, 0, :], cos_t).then_inc(w_in, 16)
                    sp.dma_start(cos_sin[:, :, 1, :], sin_t).then_inc(w_in, 16)
                    sp.wait_ge(w_in, 96)

                @block.gpsimd
                def _(pool):
                    for j in range(PAIRS):
                        pool.wait_ge(w_his, j + 1)
                        pool.tensor_tensor(w_lo[:, j, :], w_all[:, j, :], w_hi[:, j, :].bitcast(F32),
                                           ALU.subtract).then_inc(w_los, 1)
                    pool.wait_ge(w_los, PAIRS)

                @block.vector
                def _(dve):
                    moments.by_dve(dve, None)
                    for g in range(GROUPS + 1):
                        if g < GROUPS:
                            wait(dve, xt_psum, g - 1)
                            for t in range(4):
                                n = g * 4 + t
                                one = dve.tensor_scalar(xn[g % 2][:, t, :], X[:, n, :], mean[:, n:n + 1],
                                                        rstd[:, n:n + 1], ALU.subtract, ALU.mult)
                            one.then_inc(xn_ready, 1)
                        if g > 0:
                            k = (g - 1) % 2
                            dve.wait_ge(hi_ready, g)
                            cols = slice((g - 1) * 512, g * 512)
                            dve.tensor_tensor(XT[:, 1, cols], bank[k][:, :], XT[:, 0, cols].bitcast(F32),
                                              ALU.subtract).then_inc(lo_ready, 1)

                @block.scalar
                def _(act):
                    moments.by_act(act)
                    act.wait_ge(w_in, 96)
                    for g in range(GROUPS):
                        act.wait_ge(xt_psum, g + 1)
                        act.activation(XT[:, 0, g * 512:(g + 1) * 512], bank[g % 2][:, :],
                                       ACT.Copy).then_inc(hi_ready, 1)
                        for j in range(g * PAIRS // GROUPS, (g + 1) * PAIRS // GROUPS):
                            act.activation(w_hi[:, j, :], w_all[:, j, :], ACT.Copy).then_inc(w_his, 1)

                @block.tensor
                def _(pe):
                    for g in range(GROUPS):
                        pe.wait_ge(xn_ready, g + 1)
                        wait(pe, lo_ready, g - 1)
                        for t in range(4):
                            one = pe.transpose(bank[g % 2][:, t * P:(t + 1) * P], xn[g % 2][:, t, :], ident[:, :])
                        one.then_inc(xt_psum, 1)

        xs = sb("xs", [P, 2, 512], F32R)
        turned = [sb(f"turned{k}", [P, 2, 4, HEAD_DIM]) for k in range(2)]
        R = sb("R", [P, 4, 2, P])
        QT = [sb(f"QT{k}", [P, 512]) for k in range(2)]
        KT = [[sb(f"KT{k}{h}", [P, 512]) for h in range(2)] for k in range(2)]
        v_new = sb("v_new", [P, 4, P])
        V = [sb(f"V{k}", [P, 4, P]) for k in range(2)]
        prob = [sb(f"prob{k}", [P, 2, 512]) for k in range(2)]
        probT = [sb(f"probT{k}", [P, 2, 4, P]) for k in range(2)]
        OT = sb("OT", [P, 512])
        mx = sb("mx", [P, 4])
        nb = sb("nb", [P, 4])
        sums = sb("sums", [P, 4])
        rec = sb("rec", [P, 4])
        pt_bank, o_bank, misc = bank[0:2], bank[2], bank[3]
        spare = [s_bank[k][:, 1, :] for k in range(2)]

        def score_area(q):
            n = (q + 1) * P
            if q < 2:
                return s_bank[q][:, 0, 0:2 * n].rearrange("p (h c) -> p h c", h=2)
            return s_bank[q - 2][:, :, 0:n]

        def project_area(t):
            return (spare[0], misc)[t % 2]


        kt_zero = sem("kt_zero")
        xs_in = sem("xs_in")
        qkv_psum = sem("qkv_psum")
        rope_ready = sem("rope_ready")
        v_ready = sem("v_ready")
        v_moved = sem("v_moved")
        r_ready = sem("r_ready")
        qt_psum = sem("qt_psum")
        kt_psum = sem("kt_psum")
        qt_ready = sem("qt_ready")
        kt_ready = sem("kt_ready")
        s_psum = sem("s_psum")
        mx_ready = sem("mx_ready")
        nb_ready = sem("nb_ready")
        exp_ready = sem("exp_ready")
        rec_ready = sem("rec_ready")
        prob_ready = sem("prob_ready")
        pt_psum = sem("pt_psum")
        ptA_ready = sem("ptA_ready")
        ptB_ready = sem("ptB_ready")
        pv_psum = sem("pv_psum")
        ot_ready = sem("ot_ready")
        y_psum = sem("y_psum")
        y_used = sem("y_used")
        pt_ready = (ptA_ready, ptB_ready)

        def program(eng, step):
            for i in (-1, 0, 1):
                step(eng, i, i % 2)
            with eng.Fori(0, (STEPS - 4) // 4) as k:
                for s in range(4):
                    step(eng, k * 4 + 2 + s, s % 2)
            for i in (STEPS - 2, STEPS - 1, STEPS):
                step(eng, i, i % 2)

        def has(i, j):
            return not isinstance(i, int) or 0 <= i + j < STEPS

        with nc.Block() as block:
            @block.sync
            def _(sp):
                def step(sp, i, kk):
                    if has(i, 1):
                        wait(sp, qkv_psum, 4 * i + 4)
                        g = (i + 1) // PAIRS
                        sp.dma_start(xs[:, :, :].bitcast(F32),
                                     XT[:, :, bass.ds(g * 512, 512)].bitcast(F32)).then_inc(xs_in, 16)
                        sp.wait_ge(v_ready, 4 * i + 8)
                        wait(sp, pv_psum, 4 * i)
                        sp.dma_start(V[1 - kk][:, :, :], v_new[:, :, :]).then_inc(v_moved, 16)
                program(sp, step)
                sp.wait_ge(xs_in, 16 * STEPS)
                sp.wait_ge(v_moved, 16 * STEPS)

            @block.gpsimd
            def _(pool):
                for k in range(2):
                    pool.memset(KT[k][0][64:128, :], 0.0).then_inc(kt_zero, 1)
                    pool.memset(KT[k][1][0:64, :], 0.0).then_inc(kt_zero, 1)

                def step(pool, i, kk):
                    if has(i, 1):
                        wait(pool, kt_psum, i + 1)
                        for t in range(4):
                            pool.wait_ge(rope_ready, 4 * (i + 1) + t + 1)
                            o = R[:, t, :, :].rearrange("p a (c two) -> p (a c) two", two=2)
                            a = turned[t % 2][:, 0, :, :].rearrange("p h (c two) -> p (h c) two", two=2)
                            b = turned[t % 2][:, 1, :, :].rearrange("p h (c two) -> p (h c) two", two=2)
                            for z in range(2):
                                one = pool.tensor_tensor(o[:, :, z], a[:, :, z], b[:, :, 1 - z], ALU.add)
                            one.then_inc(r_ready, 1)
                program(pool, step)

            @block.tensor
            def _(pe):
                def project(i, t):
                    if t == 0:
                        pe.wait_ge(xs_in, 16 * i + 16)
                        wait(pe, exp_ready, 8 * (i - 1) - 2)
                    elif t == 1:
                        wait(pe, y_used, i - 2)
                        wait(pe, kt_ready, i)
                    else:
                        pe.wait_ge(v_ready, 4 * i + t - 1)
                    j = i % PAIRS
                    hi, lo = xs[:, 0, t * P:(t + 1) * P], xs[:, 1, t * P:(t + 1) * P]
                    wh = w_hi[:, bass.ds(j, 1), :].rearrange("p a c -> p (a c)")
                    wl = w_lo[:, bass.ds(j, 1), :].rearrange("p a c -> p (a c)")
                    o = project_area(t)[:, 0:QKV]
                    pe.matmul(o, hi, wh, start=True, stop=False)
                    pe.matmul(o, hi, wl, start=False, stop=False)
                    pe.matmul(o, lo, wh, start=False, stop=True).then_inc(qkv_psum, 1)

                def turn(i, which):
                    if which == 0:
                        pe.wait_ge(r_ready, 4 * i + 4)
                        wait(pe, exp_ready, 8 * (i - 1))
                    else:
                        pe.wait_ge(v_ready, 4 * i + 4)
                    o = (spare[1], misc)[which]
                    for t in range(4):
                        one = pe.transpose(o[:, t * P:(t + 1) * P], R[:, t, which, :], ident[:, :])
                    one.then_inc((qt_psum, kt_psum)[which], 1)

                def scores(i, kk, q):
                    if q == 0:
                        pe.wait_ge(kt_ready, i + 1)
                    wait(pe, exp_ready, 2 * (4 * i + q) - 2)
                    if has(i, 1):
                        if q == 2:
                            pe.wait_ge(v_ready, 4 * (i + 1) + 3)
                        if q == 3:
                            pe.wait_ge(qt_ready, i + 2)
                    n = (q + 1) * P
                    area = score_area(q)
                    for h in range(2):
                        pe.matmul(area[:, h, 0:n], QT[kk][:, q * P:n], KT[kk][h][:, 0:n],
                                  start=True, stop=False)
                        one = pe.matmul(area[:, h, q * P:n], identb[:, :], causal[:, :],
                                        start=False, stop=True)
                    one.then_inc(s_psum, 1)

                def turn_probs(i, q):
                    Q = 4 * i + q
                    pe.wait_ge(prob_ready, Q + 1)
                    for h in range(2):
                        wait(pe, pt_ready[h], Q)
                        for b in range(q + 1):
                            one = pe.transpose(pt_bank[h][:, b * P:(b + 1) * P],
                                               prob[q % 2][:, h, b * P:(b + 1) * P], ident[:, :])
                        one.then_inc(pt_psum, 1)

                def weigh(i, kk, q):
                    if q == 0:
                        pe.wait_ge(v_moved, 16 * i + 16)
                        wait(pe, ot_ready, i)
                    pe.wait_ge(ptA_ready, 4 * i + q + 1)
                    pe.wait_ge(ptB_ready, 4 * i + q + 1)
                    for b in range(q + 1):
                        for h in range(2):
                            one = pe.matmul(o_bank[64 * h:64 * h + 64, q * P:(q + 1) * P],
                                            V[kk][:, b, 64 * h:64 * h + 64],
                                            probT[q % 2][:, h, b, :], start=(b == 0), stop=(b == q))
                    one.then_inc(pv_psum, 1)

                def out_project(i, last):
                    pe.wait_ge(ot_ready, i + 1)
                    if last:
                        wait(pe, y_used, i)
                    else:
                        pe.wait_ge(kt_ready, i + 3)
                    j = i % PAIRS
                    for t in range(4):
                        one = pe.matmul(misc[:, t * P:(t + 1) * P], OT[:, t * P:(t + 1) * P],
                                        wo[:, bass.ds(j, 1), :].rearrange("p a c -> p (a c)"),
                                        start=True, stop=True)
                    one.then_inc(y_psum, 1)

                def step(pe, i, kk):
                    last, this, following = has(i, -1), has(i, 0), has(i, 1)
                    if last:
                        turn_probs(i - 1, 2)
                    if this:
                        scores(i, kk, 0)
                    if following:
                        project(i + 1, 0)
                        project(i + 1, 1)
                    if last:
                        weigh(i - 1, 1 - kk, 2)
                        turn_probs(i - 1, 3)
                    if this:
                        scores(i, kk, 1)
                    if following:
                        project(i + 1, 2)
                        project(i + 1, 3)
                    if last:
                        weigh(i - 1, 1 - kk, 3)
                    if this:
                        turn_probs(i, 0)
                        scores(i, kk, 2)
                    if following:
                        turn(i + 1, 0)
                    if this:
                        turn_probs(i, 1)
                        weigh(i, kk, 0)
                    if following:
                        turn(i + 1, 1)
                    if this:
                        scores(i, kk, 3)
                        weigh(i, kk, 1)
                    if last:
                        out_project(i - 1, not following)
                pe.wait_ge(kt_zero, 4)
                program(pe, step)

            @block.vector
            def _(dve):
                def rope(i, t):
                    dve.wait_ge(qkv_psum, 4 * i + t + 1)
                    wait(dve, r_ready, 4 * i + t - 1)
                    qk = project_area(t)[:, 0:4 * HEAD_DIM].rearrange("p (a h c) -> p a h c", a=1, h=4)
                    table = cos_sin[:, t, :, :].rearrange("p s (a c) -> p s a c", a=1)
                    shape = [P, 2, 4, HEAD_DIM]
                    dve.tensor_tensor(turned[t % 2][:, :, :, :], qk.to_broadcast(shape), table.to_broadcast(shape),
                                      ALU.mult).then_inc(rope_ready, 1)

                def maximum(i, q):
                    Q = 4 * i + q
                    c = 2 * (q % 2)
                    dve.wait_ge(s_psum, Q + 1)
                    dve.reduce_max(mx[:, c:c + 2], score_area(q), AX).then_inc(mx_ready, 1)
                    dve.wait_ge(mx_ready, Q + 1)
                    dve.tensor_scalar(nb[:, c:c + 2], mx[:, c:c + 2], -SCALE, None, ALU.mult).then_inc(nb_ready, 1)

                def normalise(i, q):
                    Q = 4 * i + q
                    c = 2 * (q % 2)
                    dve.wait_ge(exp_ready, 2 * Q + 2)
                    dve.reciprocal(rec[:, c:c + 2], sums[:, c:c + 2]).then_inc(rec_ready, 1)
                    dve.wait_ge(rec_ready, Q + 1)
                    for h in range(2):
                        w = prob[q % 2][:, h, 0:(q + 1) * P]
                        one = dve.tensor_scalar(w, w, rec[:, c + h:c + h + 1], None, ALU.mult)
                    one.then_inc(prob_ready, 1)

                def copy_b(i, q):
                    dve.wait_ge(pt_psum, 2 * (4 * i + q) + 2)
                    wait(dve, pv_psum, 4 * i + q - 1)
                    dve.tensor_copy(probT[q % 2][:, 1, 0:q + 1, :],
                                    pt_bank[1][:, 0:(q + 1) * P].rearrange("p (b r) -> p b r", r=P)
                                    ).then_inc(ptB_ready, 1)

                def residual(i):
                    dve.wait_ge(y_psum, i + 1)
                    wait(dve, y_used, i)
                    tok = X[:, bass.ds((i // PAIRS) * 4, 4), :]
                    dve.tensor_tensor(tok, misc[:, :].rearrange("p (t d) -> p t d", t=4), tok,
                                      ALU.add).then_inc(y_used, 1)

                def step(dve, i, kk):
                    last, this, following = has(i, -1), has(i, 0), has(i, 1)
                    if last:
                        copy_b(i - 1, 2)
                    if this:
                        maximum(i, 0)
                    if last:
                        normalise(i - 1, 3)
                    if this:
                        normalise(i, 0)
                    if following:
                        rope(i + 1, 0)
                        rope(i + 1, 1)
                    if last:
                        copy_b(i - 1, 3)
                    if this:
                        maximum(i, 1)
                    if following:
                        rope(i + 1, 2)
                        rope(i + 1, 3)
                    if this:
                        copy_b(i, 0)
                        normalise(i, 1)
                        maximum(i, 2)
                        copy_b(i, 1)
                        normalise(i, 2)
                        maximum(i, 3)
                    if last:
                        residual(i - 1)
                program(dve, step)

            @block.scalar
            def _(act):
                def values(i, t):
                    act.wait_ge(rope_ready, 4 * i + t + 1)
                    if t == 0:
                        wait(act, v_moved, 16 * i)
                    act.activation(v_new[:, t, :], project_area(t)[:, 2 * P:3 * P], ACT.Copy).then_inc(v_ready, 1)

                def exponent(i, q):
                    Q = 4 * i + q
                    act.wait_ge(nb_ready, Q + 1)
                    n = (q + 1) * P
                    for h in range(2):
                        c = 2 * (q % 2) + h
                        wait(act, pt_psum, 2 * Q - 3 + h)
                        act.activation(prob[q % 2][:, h, 0:n], score_area(q)[:, h, :], ACT.Exp,
                                       bias=nb[:, c:c + 1], scale=SCALE,
                                       accum_out=sums[:, c:c + 1]).then_inc(exp_ready, 1)

                def copy_a(i, q):
                    act.wait_ge(pt_psum, 2 * (4 * i + q) + 1)
                    wait(act, pv_psum, 4 * i + q - 1)
                    act.activation(probT[q % 2][:, 0, 0:q + 1, :],
                                   pt_bank[0][:, 0:(q + 1) * P].rearrange("p (b r) -> p b r", r=P),
                                   ACT.Copy).then_inc(ptA_ready, 1)

                def queries(i, kk):
                    act.wait_ge(qt_psum, i + 1)
                    wait(act, s_psum, 4 * (i - 1))
                    act.activation(QT[kk][:, :], spare[1], ACT.Copy).then_inc(qt_ready, 1)

                def keys(i, kk):
                    act.wait_ge(kt_psum, i + 1)
                    wait(act, s_psum, 4 * (i - 1))
                    act.activation(KT[kk][0][0:64, :], misc[0:64, :], ACT.Copy)
                    act.activation(KT[kk][1][64:128, :], misc[64:128, :], ACT.Copy).then_inc(kt_ready, 1)

                def outputs(i):
                    act.wait_ge(pv_psum, 4 * i + 4)
                    wait(act, y_psum, i)
                    act.activation(OT[:, :], o_bank[:, :], ACT.Copy).then_inc(ot_ready, 1)

                def step(act, i, kk):
                    last, this, following = has(i, -1), has(i, 0), has(i, 1)
                    if last:
                        copy_a(i - 1, 2)
                    if this:
                        exponent(i, 0)
                    if following:
                        values(i + 1, 0)
                        values(i + 1, 1)
                    if last:
                        copy_a(i - 1, 3)
                    if following:
                        values(i + 1, 2)
                    if this:
                        exponent(i, 1)
                    if following:
                        values(i + 1, 3)
                    if last:
                        outputs(i - 1)
                    if this:
                        copy_a(i, 0)
                    if following:
                        queries(i + 1, 1 - kk)
                    if this:
                        copy_a(i, 1)
                        exponent(i, 2)
                    if following:
                        keys(i + 1, 1 - kk)
                    if this:
                        exponent(i, 3)
                program(act, step)


def kernel(**inputs):
    import concourse.bacc as bacc
    from concourse.bass_utils import run_bass_kernel_spmd

    x = np.ascontiguousarray(inputs["L0_attn_x"])
    batch, seq, dim = x.shape
    half = np.arange(0, HEAD_DIM, 2)
    freqs = (np.float32(1.0) / np.float32(10000.0) ** (half / HEAD_DIM).astype(np.float32)).astype(np.float32)
    angles = (np.arange(seq).astype(np.float32)[:, None] * freqs[None, :]).astype(np.float32)
    cos = np.repeat(np.cos(angles), 2, axis=1).astype(np.float32)
    sin = np.repeat(np.sin(angles), 2, axis=1).astype(np.float32) * np.tile(np.float32([1, -1]), HEAD_DIM // 2)
    by_position = lambda t: np.ascontiguousarray(t.reshape(seq // P, P, HEAD_DIM).transpose(1, 0, 2))
    down = inputs["L0_ffn_down_w"]
    E, D, F = down.shape
    arrays = {
        "x": x.reshape(batch * seq, dim),
        "w_qkv": np.ascontiguousarray(inputs["L0_attn_W_qkv"]),
        "w_out": np.ascontiguousarray(inputs["L0_attn_W_out"]),
        "router_t": np.ascontiguousarray(inputs["L0_ffn_router_w"].T),
        "gate_t": np.ascontiguousarray(inputs["L0_ffn_gate_w"].transpose(2, 0, 1)),
        "up_t": np.ascontiguousarray(inputs["L0_ffn_up_w"].transpose(2, 0, 1)),
        "down_t": np.ascontiguousarray(down.reshape(E, D, F // P, P).transpose(3, 0, 2, 1)),
        "cos_t": by_position(cos),
        "sin_t": by_position(sin),
    }
    nc = bacc.Bacc("TRN2", target_bir_lowering=False, num_devices=1)
    args = [nc.dram_tensor(k, a.shape, mybir.dt.from_np(a.dtype), kind="ExternalInput").ap()
            for k, a in arrays.items()]
    out = nc.dram_tensor("out", (batch * seq, dim), F32, kind="ExternalOutput").ap()
    macaron(nc, *args, out)
    r = run_bass_kernel_spmd(nc, [arrays], core_ids=[0])
    return r.results[0]["out"].reshape(batch, seq, dim)
```
